# Optimizing a Trainium2 kernel written in Bass

```python
import numpy as np
import jax
import jax.numpy as jnp

def _softmax(x, axis=-1):
    return jax.nn.softmax(x, axis=axis)

def _gelu(x):
    return jax.nn.gelu(x, approximate=True)

def _silu(x):
    return jax.nn.silu(x)

def _sigmoid(x):
    return jax.nn.sigmoid(x)

def _layernorm(x, axis=-1, eps=1e-05):
    m = jnp.mean(x, axis=axis, keepdims=True)
    v = jnp.var(x, axis=axis, keepdims=True)
    return (x - m) / jnp.sqrt(v + eps)

def _scatter_add(tgt, idx, src, axis=0):
    return tgt.at[idx].add(src)

def _segment_sum(src, seg, n):
    return jax.ops.segment_sum(src, seg, n)
kernel_name = 'mk_audio_tower_d2_tok_audfeat256_r4_c14132'

def setup_inputs(seed: int=0):
    np.random.seed(seed)
    _w = jnp.asarray

    def _rec_inputs():
        import jax
        import jax.numpy as jnp
        _rk = jax.random.key(seed)
        x = 7.22013e-05 + 1.00017 * jax.random.normal(jax.random.fold_in(_rk, 1), (128, 125, 128), jnp.float32)
        return x
    x = _rec_inputs()

    def _L0_tok_setup():
        import jax, jax.numpy as jnp
        import numpy as np
        FILTER_SIZE = 8
        INPUT_DIM = 128
        KERNEL_SIZE = 64
        key = jax.random.key(seed)
        k1, k2, k3, k4 = jax.random.split(key, 4)
        user_batch = jax.random.normal(k1, (32, 512, INPUT_DIM), dtype=jnp.float32)
        filt = jax.random.uniform(k2, (FILTER_SIZE, INPUT_DIM), dtype=jnp.float32)
        W_k = jax.random.uniform(k3, (FILTER_SIZE * INPUT_DIM, KERNEL_SIZE), dtype=jnp.float32)
        b_k = jax.random.uniform(k4, (KERNEL_SIZE,), dtype=jnp.float32)
        return {'user_batch': user_batch, 'filt': filt, 'W_k': W_k, 'b_k': b_k}
    _L0_tok_all = _L0_tok_setup()
    _L0_tok_in = {k: v for k, v in _L0_tok_all.items() if k in ('filt', 'W_k', 'b_k')}
    del _L0_tok_all

    def _L0_attn_setup():
        import jax, jax.numpy as jnp
        import numpy as np
        from jax import lax

        def _scan_combine(c1, c2):
            a1, b1 = c1
            a2, b2 = c2
            return (a1 * a2, a2 * b1 + b2)
        key = jax.random.key(seed)
        ks = jax.random.split(key, 6)
        B, L, Cin, N, Cout = (4, 1024, 64, 128, 64)
        s = 0.02
        return {'x': jax.random.normal(ks[0], (B, L, Cin), dtype=jnp.float32), 'Wx': jax.random.normal(ks[1], (Cin, N), dtype=jnp.float32) * s, 'bx': jnp.zeros((N,), dtype=jnp.float32), 'Wbc': jax.random.normal(ks[2], (Cin, 2 * N), dtype=jnp.float32) * s, 'bbc': jnp.zeros((2 * N,), dtype=jnp.float32), 'Wd': jax.random.normal(ks[3], (Cin, N), dtype=jnp.float32) * s, 'bd': jnp.zeros((N,), dtype=jnp.float32), 'Wy': jax.random.normal(ks[4], (N, Cout), dtype=jnp.float32) * s, 'by': jnp.zeros((Cout,), dtype=jnp.float32)}
    _L0_attn_all = _L0_attn_setup()
    _L0_attn_in = {k: v for k, v in _L0_attn_all.items() if k in ('Wx', 'bx', 'Wbc', 'bbc', 'Wd', 'bd', 'Wy', 'by')}
    del _L0_attn_all

    def _L0_ffn_setup():
        import jax, jax.numpy as jnp
        import numpy as np
        B, H, E, IN, OUT = (1024, 1, 8, 64, 64)

        @jax.custom_vjp
        def bin_active(x):
            return jnp.sign(x)

        def _ba_fwd(x):
            return (jnp.sign(x), x)

        def _ba_bwd(x, g):
            return (g * (jnp.abs(x) <= 1.0).astype(g.dtype),)
        bin_active.defvjp(_ba_fwd, _ba_bwd)

        @jax.custom_vjp
        def bin_gate(x):
            return (x > 0.5).astype(x.dtype)

        def _bg_fwd(x):
            return ((x > 0.5).astype(x.dtype), None)

        def _bg_bwd(_, g):
            return (g,)
        bin_gate.defvjp(_bg_fwd, _bg_bwd)
        key = jax.random.key(seed)
        k1, k2, k3, k4, k5 = jax.random.split(key, 5)
        x = jax.random.normal(k1, (B, H, IN), dtype=jnp.float32)
        weight = jax.random.normal(k2, (H, E, IN, OUT), dtype=jnp.float32) * 0.05
        proj_w = jax.random.normal(k3, (E, IN), dtype=jnp.float32) * 0.05
        proj_b = jax.random.normal(k4, (E,), dtype=jnp.float32) * 0.05
        scale = jax.random.normal(k5, (H, 1, OUT), dtype=jnp.float32) * 0.1
        return {'x': x, 'weight': weight, 'proj_w': proj_w, 'proj_b': proj_b, 'scale': scale}
    _L0_ffn_all = _L0_ffn_setup()
    _L0_ffn_in = {k: v for k, v in _L0_ffn_all.items() if k in ('weight', 'proj_w', 'proj_b', 'scale')}
    del _L0_ffn_all

    def _L1_attn_setup():
        import jax, jax.numpy as jnp
        import numpy as np
        import math
        PI = math.pi

        def _encode_phase(x, w1, b1, w2, b2):
            h = jnp.tanh(jnp.einsum('bld,ed->ble', x, w1) + b1)
            return jnp.tanh(jnp.einsum('bld,kd->blk', h, w2) + b2) * PI
        key = jax.random.key(seed)
        ks = jax.random.split(key, 12)
        B, L, D, K = (2, 512, 64, 32)
        s = 0.02
        return {'x': jax.random.normal(ks[0], (B, L, D), dtype=jnp.float32), 'kw1': jax.random.normal(ks[1], (D, D), dtype=jnp.float32) * s, 'kb1': jnp.zeros((D,), dtype=jnp.float32), 'kw2': jax.random.normal(ks[2], (K, D), dtype=jnp.float32) * s, 'kb2': jnp.zeros((K,), dtype=jnp.float32), 'qw1': jax.random.normal(ks[3], (D, D), dtype=jnp.float32) * s, 'qb1': jnp.zeros((D,), dtype=jnp.float32), 'qw2': jax.random.normal(ks[4], (K, D), dtype=jnp.float32) * s, 'qb2': jnp.zeros((K,), dtype=jnp.float32), 'vw': jax.random.normal(ks[5], (D, D), dtype=jnp.float32) * s, 'vb': jnp.zeros((D,), dtype=jnp.float32)}
    _L1_attn_all = _L1_attn_setup()
    _L1_attn_in = {k: v for k, v in _L1_attn_all.items() if k in ('kw1', 'kb1', 'kw2', 'kb2', 'qw1', 'qb1', 'qw2', 'qb2', 'vw', 'vb')}
    del _L1_attn_all

    def _L1_ffn_setup():
        import jax, jax.numpy as jnp
        import numpy as np
        C = 64
        HID = 256
        E = 8
        TEMP = 1.0
        key = jax.random.key(seed)
        ks = jax.random.split(key, 7)
        x = jax.random.normal(ks[0], (8, 4096, C), dtype=jnp.float32)
        W1 = jax.random.normal(ks[1], (C, HID), dtype=jnp.float32) * 0.02
        b1 = jnp.zeros((HID,), dtype=jnp.float32)
        Wg = jax.random.normal(ks[2], (HID, E), dtype=jnp.float32) * 0.02
        bg = jnp.zeros((E,), dtype=jnp.float32)
        Wd = jax.random.normal(ks[3], (E, HID, C), dtype=jnp.float32) * 0.02
        bd = jnp.zeros((E, C), dtype=jnp.float32)
        return {'x': x, 'W1': W1, 'b1': b1, 'Wg': Wg, 'bg': bg, 'Wd': Wd, 'bd': bd}
    _L1_ffn_all = _L1_ffn_setup()
    _L1_ffn_in = {k: v for k, v in _L1_ffn_all.items() if k in ('W1', 'b1', 'Wg', 'bg', 'Wd', 'bd')}
    del _L1_ffn_all
    return {'x': x, 'L0_tok_filt': _L0_tok_in['filt'], 'L0_tok_W_k': _L0_tok_in['W_k'], 'L0_tok_b_k': _L0_tok_in['b_k'], 'L0_attn_Wx': _L0_attn_in['Wx'], 'L0_attn_bx': _L0_attn_in['bx'], 'L0_attn_Wbc': _L0_attn_in['Wbc'], 'L0_attn_bbc': _L0_attn_in['bbc'], 'L0_attn_Wd': _L0_attn_in['Wd'], 'L0_attn_bd': _L0_attn_in['bd'], 'L0_attn_Wy': _L0_attn_in['Wy'], 'L0_attn_by': _L0_attn_in['by'], 'L0_ffn_weight': _L0_ffn_in['weight'], 'L0_ffn_proj_w': _L0_ffn_in['proj_w'], 'L0_ffn_proj_b': _L0_ffn_in['proj_b'], 'L0_ffn_scale': _L0_ffn_in['scale'], 'L1_attn_kw1': _L1_attn_in['kw1'], 'L1_attn_kb1': _L1_attn_in['kb1'], 'L1_attn_kw2': _L1_attn_in['kw2'], 'L1_attn_kb2': _L1_attn_in['kb2'], 'L1_attn_qw1': _L1_attn_in['qw1'], 'L1_attn_qb1': _L1_attn_in['qb1'], 'L1_attn_qw2': _L1_attn_in['qw2'], 'L1_attn_qb2': _L1_attn_in['qb2'], 'L1_attn_vw': _L1_attn_in['vw'], 'L1_attn_vb': _L1_attn_in['vb'], 'L1_ffn_W1': _L1_ffn_in['W1'], 'L1_ffn_b1': _L1_ffn_in['b1'], 'L1_ffn_Wg': _L1_ffn_in['Wg'], 'L1_ffn_bg': _L1_ffn_in['bg'], 'L1_ffn_Wd': _L1_ffn_in['Wd'], 'L1_ffn_bd': _L1_ffn_in['bd']}

def reference(x, L0_tok_filt, L0_tok_W_k, L0_tok_b_k, L0_attn_Wx, L0_attn_bx, L0_attn_Wbc, L0_attn_bbc, L0_attn_Wd, L0_attn_bd, L0_attn_Wy, L0_attn_by, L0_ffn_weight, L0_ffn_proj_w, L0_ffn_proj_b, L0_ffn_scale, L1_attn_kw1, L1_attn_kb1, L1_attn_kw2, L1_attn_kb2, L1_attn_qw1, L1_attn_qb1, L1_attn_qw2, L1_attn_qb2, L1_attn_vw, L1_attn_vb, L1_ffn_W1, L1_ffn_b1, L1_ffn_Wg, L1_ffn_bg, L1_ffn_Wd, L1_ffn_bd):
    import jax
    import jax.numpy as jnp

    def _L0_tok_ref(user_batch, filt, W_k, b_k):
        import jax, jax.numpy as jnp
        import numpy as np
        FILTER_SIZE = 8
        INPUT_DIM = 128
        KERNEL_SIZE = 64
        B, L, D = user_batch.shape
        F = filt.shape[0]
        n_win = L - F
        idx = jnp.arange(n_win)[:, None] + jnp.arange(F)[None, :]
        windows = user_batch[:, idx, :]
        W = W_k.reshape(F, D, -1)
        out = jnp.einsum('blfd,fd,fdk->blk', windows, filt, W)
        return jax.nn.relu(out + b_k)

    def _L0_attn_ref(x, Wx, bx, Wbc, bbc, Wd, bd, Wy, by):
        import jax, jax.numpy as jnp
        import numpy as np
        from jax import lax

        def _scan_combine(c1, c2):
            a1, b1 = c1
            a2, b2 = c2
            return (a1 * a2, a2 * b1 + b2)
        x_proj = x @ Wx + bx
        BC = x @ Wbc + bbc
        delta = x @ Wd + bd
        Bm, C = jnp.split(BC, 2, axis=-1)
        A_bar = jnp.exp(-jax.nn.softplus(delta))
        B_bar = (1.0 - A_bar) * Bm
        u = B_bar * x_proj
        _, h = lax.associative_scan(_scan_combine, (A_bar, u), axis=1)
        y = C * h
        return y @ Wy + by

    def _L0_ffn_ref(x, weight, proj_w, proj_b, scale):
        import jax, jax.numpy as jnp
        import numpy as np
        B, H, E, IN, OUT = (1024, 1, 8, 64, 64)

        @jax.custom_vjp
        def bin_active(x):
            return jnp.sign(x)

        def _ba_fwd(x):
            return (jnp.sign(x), x)

        def _ba_bwd(x, g):
            return (g * (jnp.abs(x) <= 1.0).astype(g.dtype),)
        bin_active.defvjp(_ba_fwd, _ba_bwd)

        @jax.custom_vjp
        def bin_gate(x):
            return (x > 0.5).astype(x.dtype)

        def _bg_fwd(x):
            return ((x > 0.5).astype(x.dtype), None)

        def _bg_bwd(_, g):
            return (g,)
        bin_gate.defvjp(_bg_fwd, _bg_bwd)
        xh = jnp.transpose(x, (1, 0, 2))
        gate = jax.nn.sigmoid(jnp.einsum('hbi,ei->hbe', xh, proj_w) + proj_b)
        gate = bin_gate(gate)
        w = jnp.einsum('hbe,heio->hbio', gate, weight)
        xb = bin_active(xh)
        wb = bin_active(w)
        y = jnp.einsum('hbi,hbio->hbo', xb, wb)
        y = y * scale
        return jnp.transpose(y, (1, 0, 2))

    def _L1_attn_ref(x, kw1, kb1, kw2, kb2, qw1, qb1, qw2, qb2, vw, vb):
        import jax, jax.numpy as jnp
        import numpy as np
        import math
        PI = math.pi

        def _encode_phase(x, w1, b1, w2, b2):
            h = jnp.tanh(jnp.einsum('bld,ed->ble', x, w1) + b1)
            return jnp.tanh(jnp.einsum('bld,kd->blk', h, w2) + b2) * PI
        B, L, D = x.shape
        key_phase = _encode_phase(x, kw1, kb1, kw2, kb2)
        query_phase = _encode_phase(x, qw1, qb1, qw2, qb2)
        K = key_phase.shape[-1]
        value = jnp.einsum('bld,ed->ble', x, vw) + vb
        cos_k = jnp.cos(key_phase)[..., None]
        sin_k = jnp.sin(key_phase)[..., None]
        v_exp = value[:, :, None, :]
        mem_real = jnp.cumsum(cos_k * v_exp, axis=1)
        mem_imag = jnp.cumsum(sin_k * v_exp, axis=1)
        cos_q = jnp.cos(query_phase)[..., None]
        sin_q = jnp.sin(query_phase)[..., None]
        retrieved = jnp.sum(mem_real * cos_q + mem_imag * sin_q, axis=2)
        positions = jnp.arange(1, L + 1, dtype=x.dtype)
        norm = jnp.sqrt(positions * K)[None, :, None]
        return retrieved / norm

    def _L1_ffn_ref(x, W1, b1, Wg, bg, Wd, bd):
        import jax, jax.numpy as jnp
        import numpy as np
        C = 64
        HID = 256
        E = 8
        TEMP = 1.0
        orig_shape = x.shape
        xf = x.reshape(-1, orig_shape[-1])
        H = jax.nn.gelu(xf @ W1 + b1, approximate=False)
        probs = jax.nn.softmax((H @ Wg + bg) / TEMP, axis=-1)
        assign = jnp.argmax(probs, axis=-1)
        out = jnp.zeros_like(xf)
        for e in range(Wd.shape[0]):
            y = H @ Wd[e] + bd[e]
            sel = (assign == e)[:, None]
            out = out + jnp.where(sel, probs[:, e:e + 1] * y, 0.0)
        return out.reshape(orig_shape)
    h = _L0_tok_ref(x, L0_tok_filt, L0_tok_W_k, L0_tok_b_k)
    h = h + _L0_attn_ref(_layernorm(h, axis=-1), L0_attn_Wx, L0_attn_bx, L0_attn_Wbc, L0_attn_bbc, L0_attn_Wd, L0_attn_bd, L0_attn_Wy, L0_attn_by)
    h = h + _L0_ffn_ref(_layernorm(h, axis=-1), L0_ffn_weight, L0_ffn_proj_w, L0_ffn_proj_b, L0_ffn_scale)
    h = h + _L1_attn_ref(_layernorm(h, axis=-1), L1_attn_kw1, L1_attn_kb1, L1_attn_kw2, L1_attn_kb2, L1_attn_qw1, L1_attn_qb1, L1_attn_qw2, L1_attn_qb2, L1_attn_vw, L1_attn_vb)
    h = h + _L1_ffn_ref(_layernorm(h, axis=-1), L1_ffn_W1, L1_ffn_b1, L1_ffn_Wg, L1_ffn_bg, L1_ffn_Wd, L1_ffn_bd)
    return h

_drawn_inputs = setup_inputs


def setup_inputs(seed=0):
    import zlib

    import numpy as np

    out = dict(_drawn_inputs(seed))
    spreads = {'L0_attn_bx': (0.0, 0.8),
     'L0_attn_bbc': (0.0, 0.8),
     'L0_attn_bd': (0.0, 0.8),
     'L0_attn_by': (0.0, 0.1),
     'L1_attn_kb1': (0.0, 0.8),
     'L1_attn_kb2': (0.0, 0.701),
     'L1_attn_qb1': (0.0, 0.8),
     'L1_attn_qb2': (0.0, 0.849),
     'L1_attn_vb': (0.0, 0.1),
     'L1_ffn_b1': (0.0, 0.8),
     'L1_ffn_bg': (0.0, 0.8),
     'L1_ffn_bd': (0.0, 0.8)}
    factors = {'L0_attn_Wx': 8.0,
     'L0_attn_Wbc': 8.0,
     'L0_attn_Wd': 8.0,
     'L0_attn_Wy': 8.0,
     'L1_attn_kw1': 8.0,
     'L1_attn_kw2': 8.0,
     'L1_attn_qw1': 8.0,
     'L1_attn_qw2': 8.0,
     'L1_ffn_W1': 8.0,
     'L1_ffn_Wg': 8.0,
     'L1_ffn_Wd': 8.0}
    for name, (base, spread) in spreads.items():
        noise = np.random.default_rng([zlib.crc32(name.encode()), seed]).standard_normal(out[name].shape)
        drawn = base * np.exp(spread * noise) if base else spread * noise
        out[name] = jnp.asarray(drawn.astype(out[name].dtype))
    for name, factor in factors.items():
        out[name] = (out[name] * factor).astype(out[name].dtype)
    return out
```

```python
import math
from contextlib import ExitStack

import numpy as np

import concourse.bass as bass
from concourse import mybir

F32 = mybir.dt.float32
BF16 = mybir.dt.bfloat16
ALU = mybir.AluOpType
ACT = mybir.ActivationFunctionType
AX = mybir.AxisListType

P = 128
BATCH, FRAMES, DIM = 128, 125, 128
TAPS = 8
LEN = FRAMES - TAPS
CH = 64
STATE = 128
EXPERTS = 8
PHASES = 32
HID = 256
SEQS = 8
CHUNKS = BATCH // SEQS
PAIRS = SEQS // 2
COLS = PAIRS * LEN
OPAIRS = CH // 2
SLOTS = OPAIRS
HALF = SLOTS // 2
ZCOLS = 480
EPS = 1e-5
GATE_AT = 1e-7

SETUP_DVE, SETUP_POOL = 6, 3

A_JOBS = ["conv", "norm1", "x0", "delta0", "b0", "c0", "x1", "delta1", "b1", "c1", "y", "norm2", "gate0", "gate1"]
B0_JOBS = ["norm3", "enc0", "key", "score0", "attend", "up00", "up10", "down0", "down2", "down4", "down6", "gateT"]
B1_JOBS = ["enc1", "value", "query", "score1", "norm4", "up01", "up11", "logits", "down1", "down3", "down5", "down7", "bias"]
BANK_OF = {j: ("A", A_JOBS.index(j), len(A_JOBS)) for j in A_JOBS}
BANK_OF |= {j: ("B0", B0_JOBS.index(j), len(B0_JOBS)) for j in B0_JOBS}
BANK_OF |= {j: ("B1", B1_JOBS.index(j), len(B1_JOBS)) for j in B1_JOBS}

PACK = [("conv_w", TAPS * CH), ("filt", TAPS), ("conv_b", CH), ("w_x", STATE), ("w_b", STATE), ("w_c", STATE),
        ("w_delta", STATE), ("b_x", 1), ("b_b", 1), ("b_c", 1), ("b_delta", 1), ("w_y", CH), ("b_y", CH),
        ("w_gate", P), ("b_gate", 1), ("scale", CH), ("w_enc", P), ("b_enc", 1), ("w_phase", 4 * P),
        ("b_key", 1), ("b_query", 1), ("w_value", CH), ("b_value", CH), ("w_up", HID), ("b_up", 2),
        ("w_route", 2 * EXPERTS), ("b_route", SEQS * EXPERTS), ("w_down", 2 * EXPERTS * CH),
        ("b_down", SEQS * CH), ("ident", P), ("causal", LEN), ("pair_sum", 2), ("fold", 1),
        ("sin_scale", 1), ("sin_bias", 1), ("rank", SEQS * EXPERTS)]
AT, _n = {}, 0
for _name, _w in PACK:
    AT[_name] = (_n, _n + _w)
    _n += _w
PACKED = _n


def value(chunk, per, k):
    i, off = chunk
    return max(i * per + off * per + k, 0) if isinstance(i, int) else i * per + (off * per + k)


def done(job, chunk):
    _, j, per = BANK_OF[job]
    return value(chunk, per, j + 1)


def before(job, chunk):
    _, j, per = BANK_OF[job]
    return value(chunk, per, j)


def tower(nc, x, params, experts, out):
    with ExitStack() as ctx:
        def sb(name, shape, dt=F32):
            return ctx.enter_context(nc.sbuf_tensor(name, shape, dt))

        def sem(name):
            return ctx.enter_context(nc.semaphore(name))

        prm = sb("prm", [P, PACKED])

        def par(name):
            return prm[:, AT[name][0]:AT[name][1]]

        taps = sb("taps", [P, TAPS, CH])
        half_bx = sb("half_bx", [P, 1])
        half_bd = sb("half_bd", [P, 1])
        signs_w = sb("signs_w", [P, OPAIRS * P], BF16)
        ew = sb("ew", [P, OPAIRS * P])
        ew_hi = sb("ew_hi", [P, OPAIRS * P], BF16)
        pair_sum = sb("pair_sum", [P, 2], BF16)
        power = sb("power", [P, SEQS])

        frames = sb("frames", [P, SEQS, FRAMES])
        conv = sb("conv", [P, SEQS, CH])
        h1 = sb("h1", [P, SEQS, CH])
        h1_by = sb("h1_by", [P, SEQS, CH])
        h2 = sb("h2", [P, SEQS, CH])
        h2_parked = sb("h2_parked", [P, SEQS, CH])
        ysum = sb("ysum", [P, SEQS, CH])
        h3 = sb("h3", [P, SEQS, CH])
        h4 = sb("h4", [P, SEQS, CH])
        h4_bias = sb("h4_bias", [P, SEQS, CH])
        h5 = sb("h5", [P, SEQS, CH])
        mixed = sb("mixed", [P, SEQS, CH])

        def norm_set(s):
            return {"sum": sb(f"sum_{s}", [P, SEQS]), "mean": sb(f"mean_{s}", [P, SEQS]),
                    "xc": sb(f"xc_{s}", [P, SEQS, CH]), "sq": sb(f"sq_{s}", [P, SEQS, CH]),
                    "ss": sb(f"ss_{s}", [P, SEQS]), "var": sb(f"var_{s}", [P, SEQS]),
                    "rstd": sb(f"rstd_{s}", [P, SEQS]), "xn": sb(f"xn_{s}", [P, SEQS, CH])}

        normA, normB = norm_set("a"), norm_set("b")
        xt1, xt2, xt3, xt4 = (sb(f"xt{n}", [P, COLS]) for n in (1, 2, 3, 4))

        xp = sb("xp", [P, COLS])
        th = sb("th", [P, COLS])
        decay = sb("decay", [P, COLS])
        bx = sb("bx", [P, COLS])
        drive = sb("drive", [P, COLS])
        state = sb("state", [P, COLS])
        yscan = sb("yscan", [P, 2, COLS])

        gates = [sb(f"gates{h}", [P, COLS], BF16) for h in (0, 1)]
        xsign = [sb(f"xsign{h}", [P, COLS], BF16) for h in (0, 1)]
        wsign = [sb(f"wsign{i}", [P, 2, COLS], BF16) for i in (0, 1)]
        prod = [sb(f"prod{i}", [P, 2, ZCOLS], BF16) for i in (0, 1)]

        enc = sb("enc", [P, 2, COLS])
        ang = sb("ang", [P, 2, COLS])
        folded = sb("folded", [P, 2, COLS])
        phase = sb("phase", [P, 2, COLS])
        val = sb("val", [P, SEQS, CH])
        score = sb("score", [P, 2, COLS])

        hid = sb("hid", [P, 2, 2, COLS])
        logit = sb("logit", [P, SEQS, EXPERTS])
        top = sb("top", [P, SEQS])
        zed = sb("zed", [P, SEQS, EXPERTS])
        equal = sb("equal", [P, SEQS, EXPERTS])
        zth = sb("zth", [P, SEQS, EXPERTS])
        order = sb("order", [P, SEQS, EXPERTS])
        first = sb("first", [P, SEQS])
        onehot = sb("onehot", [P, SEQS, EXPERTS])
        expd = sb("expd", [P, SEQS, EXPERTS])
        expr = sb("expr", [P, SEQS, EXPERTS])
        expz = sb("expz", [P, SEQS, EXPERTS])
        esum = sb("esum", [P, SEQS])
        prob = sb("prob", [P, SEQS])
        gate = sb("gate", [P, SEQS, EXPERTS])
        gate_t = sb("gate_t", [P, LEN])
        sel = [sb(f"sel{i}", [P, EXPERTS, CH]) for i in (0, 1)]
        fold4 = sb("fold4", [P, 4, CH])
        fold2 = sb("fold2", [P, 2, CH])

        bank = {b: ctx.enter_context(nc.psum_tensor(f"bank{b}", [P, 512], F32)) for b in ("A", "B0", "B1")}
        wbank = [ctx.enter_context(nc.psum_tensor(f"wbank{i}", [P, 2, 512], F32)) for i in (0, 1)]
        ybank = ctx.enter_context(nc.psum_tensor("ybank", [P, SEQS, CH], F32))

        filled = {b: sem(f"bank{b}_filled") for b in bank}
        drained = {b: sem(f"bank{b}_drained") for b in bank}
        params_landed, experts_landed = sem("params_landed"), sem("experts_landed")
        x_landed, stored = sem("x_landed"), sem("stored")
        ew_zeroed, setup_pool, setup_dve, setup_act = sem("ew_zeroed"), sem("setup_pool"), sem("setup_dve"), sem("setup_act")
        h1_ready, h1_by_ready = sem("h1_ready"), sem("h1_by_ready")
        norm_dve = {n: sem(f"norm{n}_dve") for n in (1, 2, 3, 4)}
        norm_pool = {n: sem(f"norm{n}_pool") for n in (1, 2, 3, 4)}
        norm_act = {n: sem(f"norm{n}_act") for n in (1, 2, 3, 4)}
        decay_ready, drive_ready, scanned = sem("decay_ready"), sem("drive_ready"), sem("scanned")
        w_filled, wsign_ready, prod_ready, prod_summed = sem("w_filled"), sem("wsign_ready"), sem("prod_ready"), sem("prod_summed")
        xsign_ready, ysum_ready = sem("xsign_ready"), sem("ysum_ready")
        h3_ready, h2_parked_ready = sem("h3_ready"), sem("h2_parked_ready")
        value_even_done = sem("value_even_done")
        folded_ready, phase_ready = sem("folded_ready"), sem("phase_ready")
        route_dve, route_act = sem("route_dve"), sem("route_act")
        mixed_ready, h5_ready = sem("mixed_ready"), sem("h5_ready")
        waits_passed = sem("waits_passed")

        def stand_alone(eng):
            eng.sem_inc(waits_passed, 1)

        def fills(job):
            return filled[BANK_OF[job][0]]

        def drains(job):
            return drained[BANK_OF[job][0]]

        def ps(job):
            return bank[BANK_OF[job][0]]

        def tok(t):
            return t[0:LEN]

        def tok_ps(job):
            return ps(job)[0:LEN, :].rearrange("p (s c) -> p s c", s=SEQS)

        def over_ch(col, n=CH):
            return col[0:LEN, :].unsqueeze(2).broadcast_to([LEN, SEQS, n])

        def over_seq(name, n=CH):
            return par(name)[0:LEN, :].unsqueeze(1).broadcast_to([LEN, SEQS, n])

        def rows(h):
            return slice(CH * h, CH * h + CH)

        def cols(p):
            return slice(p * LEN, p * LEN + LEN)

        block = ctx.enter_context(nc.Block())

        def schedule(eng, iteration):
            iteration(-1, True, False, False)
            iteration(0, True, True, False)
            with eng.Fori(1, CHUNKS - 1) as c:
                iteration(c, True, True, True)
            iteration(CHUNKS - 1, False, True, True)
            iteration(CHUNKS, False, False, True)

        @block.sync
        def _(sp):
            sp.dma_start(prm[:, :], params).then_inc(params_landed, 16)
            sp.wait_ge(ew_zeroed, 1)
            for part in range(3):
                sp.dma_start(ew[32 * part:32 * part + EXPERTS, :], experts).then_inc(experts_landed, 16)

            def iteration(c, has_a, has_f, has_b):
                if has_a:
                    if not (isinstance(c, int) and c < 0):
                        sp.wait_ge(fills("conv"), done("conv", (c, 0)))
                    sp.dma_start(frames[:, :, :], x[:, bass.ds((c + 1) * SEQS, SEQS), :]).then_inc(x_landed, 16)
                if has_b:
                    sp.wait_ge(h5_ready, value((c, -1), 1, 1))
                    sp.dma_start(out[:, bass.ds((c - 1) * SEQS, SEQS), :], h5[0:LEN, :, :]).then_inc(stored, 16)

            schedule(sp, iteration)
            sp.wait_ge(stored, 16 * CHUNKS)

        @block.tensor
        def _(pe):
            def transpose(job, chunk, n, src):
                pe.wait_ge(drains(job), before(job, chunk))
                pe.wait_ge(norm_pool[n], value(chunk, 3, 3))
                for p in range(PAIRS):
                    mm = pe.transpose(ps(job)[:, cols(p)],
                                      src["xn"][0:LEN, 2 * p:2 * p + 2, :].rearrange("t s c -> t (s c)"),
                                      par("ident")[0:LEN, 0:LEN])
                mm.then_inc(fills(job), 1)

            def project(job, chunk, h, weights, source, after):
                pe.wait_ge(drains(job), before(job, chunk))
                pe.wait_ge(drains(after), done(after, chunk))
                pe.matmul(ps(job)[:, 0:COLS], weights[rows(h), :], source[rows(h), :],
                          start=True, stop=True).then_inc(fills(job), 1)

            def a_steps(q, a):
                if 1 <= q <= SEQS:
                    s = q - 1
                    if s == 0:
                        pe.wait_ge(drains("conv"), before("conv", a))
                        pe.wait_ge(x_landed, value(a, 16, 16))
                    for f in range(TAPS):
                        mm = pe.matmul(tok_ps("conv")[:, s, :], frames[:, s, f:f + LEN], taps[:, f, :],
                                       start=(f == 0), stop=(f == TAPS - 1))
                    if s == SEQS - 1:
                        mm.then_inc(fills("conv"), 1)
                if q == 14:
                    transpose("norm1", a, 1, normA)
                for h in (0, 1):
                    for i, (job, w) in enumerate((("x", "w_x"), ("delta", "w_delta"), ("b", "w_b"), ("c", "w_c"))):
                        if q == 15 + 4 * h + i:
                            project(f"{job}{h}", a, h, par(w), xt1, "norm1")
                if q == 23:
                    pe.wait_ge(drains("y"), before("y", a))
                    for s in range(SEQS):
                        mm = pe.matmul(tok_ps("y")[:, s, :], yscan[:, s % 2, cols(s // 2)], par("w_y"),
                                       start=True, stop=True)
                    mm.then_inc(fills("y"), 1)
                if q == 28:
                    transpose("norm2", a, 2, normA)
                if q == 29:
                    project("gate0", a, 0, par("w_gate"), xt2, "norm2")

            def b_steps(q, b):
                if q == 5:
                    transpose("norm3", b, 3, normB)
                if q == 6:
                    project("enc0", b, 0, par("w_enc"), xt3, "norm3")
                    project("enc1", b, 1, par("w_enc"), xt3, "norm3")
                if q == 7:
                    pe.wait_ge(drains("value"), before("value", b))
                    for h in (0, 1):
                        for p in range(PAIRS):
                            mm = pe.matmul(tok_ps("value")[:, 2 * p + h, :], xt3[rows(h), cols(p)],
                                           par("w_value")[rows(h), :], start=True, stop=True)
                        if h == 0:
                            mm.then_inc(value_even_done, 1)
                            pe.wait_ge(value_even_done, value(b, 1, 1))
                    mm.then_inc(fills("value"), 1)
                if q == 8:
                    for i, job in enumerate(("key", "query")):
                        pe.wait_ge(drains(job), before(job, b))
                        for h in (0, 1):
                            if i == 0:
                                pe.wait_ge(drains(f"enc{h}"), done(f"enc{h}", b))
                            w = par("w_phase")[:, (2 * i + h) * P:(2 * i + h + 1) * P]
                            mm = pe.matmul(ps(job)[:, 0:COLS], w, enc[:, h, :], start=(h == 0), stop=(h == 1))
                        mm.then_inc(fills(job), 1)
                if q == 12:
                    pe.wait_ge(phase_ready, value(b, 2, 2))
                    for h in (0, 1):
                        job = f"score{h}"
                        pe.wait_ge(drains(job), before(job, b))
                        for p in range(PAIRS):
                            mm = pe.matmul(ps(job)[0:LEN, cols(p)], phase[rows(h), 0, cols(p)],
                                           phase[rows(h), 1, cols(p)], start=True, stop=True)
                        mm.then_inc(fills(job), 1)
                if q == 14:
                    pe.wait_ge(drains("attend"), before("attend", b))
                    pe.wait_ge(drains("value"), done("value", b))
                    pe.wait_ge(drains("score1"), done("score1", b))
                    for s in range(SEQS):
                        mm = pe.matmul(tok_ps("attend")[:, s, :], score[0:LEN, s % 2, cols(s // 2)], val[0:LEN, s, :],
                                       start=True, stop=True)
                    mm.then_inc(fills("attend"), 1)
                if q == 19:
                    transpose("norm4", b, 4, normB)
                for h in (0, 1):
                    if q == 20 + h:
                        for k in (0, 1):
                            project(f"up{h}{k}", b, h, par("w_up")[:, k * P:(k + 1) * P], xt4, "norm4")
                if q == 22:
                    pe.wait_ge(drains("logits"), before("logits", b))
                    pe.wait_ge(drains("up10"), done("up10", b))
                    pe.wait_ge(drains("up11"), done("up11", b))
                    lg = ps("logits")[0:LEN, 0:SEQS * EXPERTS].rearrange("p (s e) -> p s e", s=SEQS)
                    for s in range(SEQS):
                        for k in (0, 1):
                            mm = pe.matmul(lg[:, s, :], hid[:, s % 2, k, cols(s // 2)],
                                           par("w_route")[:, k * EXPERTS:(k + 1) * EXPERTS],
                                           start=(k == 0), stop=(k == 1))
                    mm.then_inc(fills("logits"), 1)
                if 23 <= q <= 30:
                    s = q - 23
                    job = f"down{s}"
                    pe.wait_ge(drains(job), before(job, b))
                    for k in (0, 1):
                        mm = pe.matmul(ps(job)[0:LEN, :], hid[:, s % 2, k, cols(s // 2)],
                                       par("w_down")[:, k * EXPERTS * CH:(k + 1) * EXPERTS * CH],
                                       start=(k == 0), stop=(k == 1))
                    mm.then_inc(fills(job), 1)
                if q == 30:
                    pe.wait_ge(drains("gateT"), before("gateT", b))
                    pe.wait_ge(route_dve, value(b, 12, 12))
                    stand_alone(pe)
                    pe.transpose(ps("gateT")[0:SEQS * EXPERTS, 0:LEN],
                                 gate[0:LEN, :, :].rearrange("t s e -> t (s e)"),
                                 par("ident")[0:LEN, 0:LEN]).then_inc(fills("gateT"), 1)
                if q == 31:
                    pe.wait_ge(drains("bias"), before("bias", b))
                    pe.wait_ge(drains("gateT"), done("gateT", b))
                    pe.matmul(ps("bias")[0:LEN, :], gate_t[0:SEQS * EXPERTS, :], par("b_down")[0:SEQS * EXPERTS, :],
                              start=True, stop=True).then_inc(fills("bias"), 1)

            def expert_weights(q, f):
                pe.wait_ge(wsign_ready, value(f, SLOTS, q - 1))
                if q % HALF == 0:
                    pe.wait_ge(drains(f"gate{q // HALF}"), done(f"gate{q // HALF}", f))
                for j in (0, 1):
                    k = 2 * (q % HALF) + j
                    mm = pe.matmul(wbank[q % 2][:, j, 0:COLS], signs_w[:, k * P:(k + 1) * P], gates[q // HALF][:, :],
                                   start=True, stop=True)
                mm.then_inc(w_filled, 1)

            def sum_products(q, f):
                pe.wait_ge(prod_ready, value(f, SLOTS, q + 1))
                if q == 0:
                    pe.wait_ge(ysum_ready, value(f, 1, 0))
                for p in range(PAIRS):
                    for j in (0, 1):
                        o = 2 * (2 * (q % HALF) + j)
                        mm = pe.matmul(ybank[:, 2 * p + q // HALF, o:o + 2], prod[q % 2][:, j, p * LEN:p * LEN + P],
                                       pair_sum[:, :], start=True, stop=True)
                mm.then_inc(prod_summed, 1)

            pe.wait_ge(params_landed, 16)
            pe.wait_ge(setup_dve, 1)

            def iteration(c, has_a, has_f, has_b):
                if has_f:
                    if isinstance(c, int) and c == 0:
                        pe.wait_ge(setup_dve, SETUP_DVE)
                        pe.wait_ge(setup_pool, SETUP_POOL)
                    expert_weights(0, (c, 0))
                    expert_weights(1, (c, 0))
                for q in range(SLOTS):
                    if has_f and q == 0:
                        project("gate1", (c, 0), 1, par("w_gate"), xt2, "norm2")
                    if has_f and 0 < q < SLOTS - 1:
                        expert_weights(q + 1, (c, 0))
                    if has_a:
                        a_steps(q, (c, 1))
                    if has_b:
                        b_steps(q, (c, -1))
                    if has_f:
                        sum_products(q, (c, 0))

            schedule(pe, iteration)

        @block.scalar
        def _(act):
            def turned(job, chunk, dst):
                act.wait_ge(fills(job), done(job, chunk))
                act.activation(dst[:, :], ps(job)[:, 0:COLS], ACT.Copy).then_inc(drains(job), 1)

            def squares(n, chunk, t):
                act.wait_ge(norm_pool[n], value(chunk, 3, 1))
                act.activation(tok(t["sq"]), tok(t["xc"]), ACT.Square).then_inc(norm_act[n], 1)

            def input_signs(h, f):
                act.wait_ge(prod_ready, value(f, SLOTS, HALF * (h + 1) - SLOTS))
                for half in (0, 1):
                    act.activation(xsign[h][rows(half), :], xt2[rows(h), :], ACT.Sign).then_inc(xsign_ready, 1)

            def a_steps(q, a):
                if q == 9:
                    act.wait_ge(drains("conv"), done("conv", a))
                    act.activation(tok(h1), tok(conv), ACT.Relu).then_inc(h1_ready, 1)
                if q == 11:
                    squares(1, a, normA)
                if q == 14:
                    turned("norm1", a, xt1)
                for h in (0, 1):
                    if q == 15 + 4 * h:
                        act.wait_ge(fills(f"x{h}"), done(f"x{h}", a))
                        act.activation(xp[:, :], ps(f"x{h}")[:, 0:COLS], ACT.Identity, bias=half_bx[:, 0:1],
                                       scale=0.5).then_inc(drains(f"x{h}"), 1)
                    if q == 16 + 4 * h:
                        act.wait_ge(fills(f"delta{h}"), done(f"delta{h}", a))
                        act.activation(th[:, :], ps(f"delta{h}")[:, 0:COLS], ACT.Tanh, bias=half_bd[:, 0:1],
                                       scale=0.5).then_inc(drains(f"delta{h}"), 1)
                if q == 25:
                    squares(2, a, normA)
                if q == 28:
                    turned("norm2", a, xt2)
                if q == 29:
                    act.wait_ge(drains("norm2"), done("norm2", a))
                    input_signs(0, a)

            def b_steps(q, b):
                if q == 2:
                    squares(3, b, normB)
                if q == 5:
                    turned("norm3", b, xt3)
                if q == 6:
                    for h in (0, 1):
                        act.wait_ge(fills(f"enc{h}"), done(f"enc{h}", b))
                        act.activation(enc[:, h, :], ps(f"enc{h}")[:, 0:COLS], ACT.Tanh,
                                       bias=par("b_enc")).then_inc(drains(f"enc{h}"), 1)
                if q == 9:
                    for i, job in enumerate(("key", "query")):
                        act.wait_ge(fills(job), done(job, b))
                        act.activation(ang[:, i, :], ps(job)[:, 0:COLS], ACT.Tanh,
                                       bias=par(f"b_{job}")).then_inc(drains(job), 1)
                if q == 11:
                    act.wait_ge(folded_ready, value(b, 2, 2))
                    for i in (0, 1):
                        act.activation(phase[:, i, :], folded[:, i, :], ACT.Sin, bias=par("sin_bias"),
                                       scale=par("sin_scale")).then_inc(phase_ready, 1)
                if q == 16:
                    squares(4, b, normB)
                if q == 19:
                    turned("norm4", b, xt4)
                for h in (0, 1):
                    if q == 20 + h:
                        for k in (0, 1):
                            act.wait_ge(fills(f"up{h}{k}"), done(f"up{h}{k}", b))
                            act.activation(hid[:, h, k, :], ps(f"up{h}{k}")[:, 0:COLS], ACT.Gelu,
                                           bias=par("b_up")[:, k:k + 1]).then_inc(drains(f"up{h}{k}"), 1)
                if q == 23:
                    act.wait_ge(route_dve, value(b, 12, 2))
                    act.activation(tok(zth), tok(zed), ACT.Tanh, scale=0.5).then_inc(route_act, 1)
                if q == 30:
                    act.wait_ge(fills("gateT"), done("gateT", b))
                    act.activation(gate_t[0:SEQS * EXPERTS, :], ps("gateT")[0:SEQS * EXPERTS, 0:LEN],
                                   ACT.Copy).then_inc(drains("gateT"), 1)

            def weight_signs(q, f):
                act.wait_ge(w_filled, value(f, SLOTS, q + 1))
                act.wait_ge(prod_ready, value(f, SLOTS, q - 1))
                act.activation(wsign[q % 2][:, :, :], wbank[q % 2][:, :, 0:COLS], ACT.Sign).then_inc(wsign_ready, 1)

            act.wait_ge(params_landed, 16)
            act.mul(half_bx[:, :], par("b_x"), 0.5).then_inc(setup_act, 1)
            act.mul(half_bd[:, :], par("b_delta"), 0.5).then_inc(setup_act, 1)
            act.wait_ge(experts_landed, 48)
            act.activation(ew_hi[:, :], ew[:, :], ACT.Copy).then_inc(setup_act, 1)
            act.wait_ge(setup_act, 3)

            def iteration(c, has_a, has_f, has_b):
                for q in range(SLOTS):
                    if has_f and q == 0:
                        input_signs(1, (c, 0))
                    if has_f:
                        weight_signs(q, (c, 0))
                    if has_a:
                        a_steps(q, (c, 1))
                    if has_b:
                        b_steps(q, (c, -1))

            schedule(act, iteration)

        @block.vector
        def _(dve):
            def sums(n, chunk, t, src):
                dve.tensor_reduce(tok(t["sum"]), tok(src), AX.X, ALU.add).then_inc(norm_dve[n], 1)
                dve.wait_ge(norm_dve[n], value(chunk, 4, 1))
                dve.tensor_scalar(tok(t["mean"]), tok(t["sum"]), 1.0 / CH, None, ALU.mult).then_inc(norm_dve[n], 1)

            def variances(n, chunk, t):
                dve.wait_ge(norm_act[n], value(chunk, 1, 1))
                dve.tensor_reduce(tok(t["ss"]), tok(t["sq"]), AX.X, ALU.add).then_inc(norm_dve[n], 1)
                dve.wait_ge(norm_dve[n], value(chunk, 4, 3))
                dve.tensor_scalar(tok(t["var"]), tok(t["ss"]), 1.0 / CH, EPS, ALU.mult, ALU.add).then_inc(norm_dve[n], 1)

            def open_gates(h, a):
                dve.wait_ge(fills(f"gate{h}"), done(f"gate{h}", a))
                dve.tensor_scalar(gates[h][:, :], ps(f"gate{h}")[:, 0:COLS], par("b_gate"), GATE_AT,
                                  ALU.add, ALU.is_gt).then_inc(drains(f"gate{h}"), 1)

            def a_steps(q, a):
                if q == 9:
                    dve.wait_ge(fills("conv"), done("conv", a))
                    dve.tensor_tensor(tok(conv), tok_ps("conv"), over_seq("conv_b"), ALU.add).then_inc(drains("conv"), 1)
                if q == 10:
                    dve.wait_ge(h1_ready, value(a, 1, 1))
                    sums(1, a, normA, h1)
                if q == 12:
                    variances(1, a, normA)
                for h in (0, 1):
                    if q == 17 + 4 * h:
                        dve.wait_ge(fills(f"b{h}"), done(f"b{h}", a))
                        dve.wait_ge(drains(f"delta{h}"), done(f"delta{h}", a))
                        dve.scalar_tensor_tensor(bx[:, :], ps(f"b{h}")[:, 0:COLS], par("b_b"), xp[:, :],
                                                 ALU.add, ALU.mult).then_inc(drains(f"b{h}"), 1)
                        dve.wait_ge(drains(f"b{h}"), done(f"b{h}", a))
                        dve.scalar_tensor_tensor(drive[:, :], th[:, :], 1.0, bx[:, :],
                                                 ALU.add, ALU.mult).then_inc(drive_ready, 1)
                        dve.wait_ge(drive_ready, value(a, 2, h + 1))
                        dve.wait_ge(decay_ready, value(a, 4, 2 * h + 2))
                        dve.tensor_tensor_scan(state[:, :], decay[:, :], drive[:, :], 0.0,
                                               ALU.mult, ALU.add).then_inc(scanned, 1)
                    if q == 18 + 4 * h:
                        dve.wait_ge(fills(f"c{h}"), done(f"c{h}", a))
                        dve.wait_ge(scanned, value(a, 2, h + 1))
                        dve.scalar_tensor_tensor(yscan[:, h, :], ps(f"c{h}")[:, 0:COLS], par("b_c"), state[:, :],
                                                 ALU.add, ALU.mult).then_inc(drains(f"c{h}"), 1)
                if q == 24:
                    dve.wait_ge(fills("y"), done("y", a))
                    dve.wait_ge(h1_by_ready, value(a, 1, 1))
                    dve.wait_ge(h2_parked_ready, value(a, 1, 0))
                    dve.tensor_tensor(tok(h2), tok_ps("y"), tok(h1_by), ALU.add).then_inc(drains("y"), 1)
                    dve.wait_ge(drains("y"), done("y", a))
                    sums(2, a, normA, h2)
                if q == 26:
                    variances(2, a, normA)
                if q == 29:
                    open_gates(0, a)

            def b_steps(q, b):
                if q == 1:
                    dve.wait_ge(h3_ready, value(b, 1, 1))
                    sums(3, b, normB, h3)
                if q == 3:
                    variances(3, b, normB)
                if q == 8:
                    dve.wait_ge(fills("value"), done("value", b))
                    dve.tensor_tensor(tok(val), tok_ps("value"), over_seq("b_value"), ALU.add).then_inc(drains("value"), 1)
                if q == 10:
                    for i, job in enumerate(("key", "query")):
                        dve.wait_ge(drains(job), done(job, b))
                        dve.scalar_tensor_tensor(folded[:, i, :], ang[:, i, :], par("fold"), ang[:, i, :],
                                                 ALU.mult, ALU.max).then_inc(folded_ready, 1)
                if q == 13:
                    for h in (0, 1):
                        dve.wait_ge(fills(f"score{h}"), done(f"score{h}", b))
                        dve.tensor_tensor(score[0:LEN, h, :].rearrange("t (p s) -> t p s", p=PAIRS),
                                          ps(f"score{h}")[0:LEN, 0:COLS].rearrange("t (p s) -> t p s", p=PAIRS),
                                          par("causal")[0:LEN, :].unsqueeze(1).broadcast_to([LEN, PAIRS, LEN]),
                                          ALU.mult).then_inc(drains(f"score{h}"), 1)
                if q == 15:
                    dve.wait_ge(fills("attend"), done("attend", b))
                    dve.tensor_tensor(tok(h4), tok_ps("attend"), tok(h3), ALU.add).then_inc(drains("attend"), 1)
                    dve.wait_ge(drains("attend"), done("attend", b))
                    sums(4, b, normB, h4)
                if q == 17:
                    variances(4, b, normB)
                if q == 23:
                    dve.wait_ge(fills("logits"), done("logits", b))
                    lg = ps("logits")[0:LEN, 0:SEQS * EXPERTS].rearrange("p (s e) -> p s e", s=SEQS)
                    dve.tensor_tensor(tok(logit), lg, par("b_route")[0:LEN, :].rearrange("p (s e) -> p s e", s=SEQS),
                                      ALU.add).then_inc(drains("logits"), 1)
                    dve.wait_ge(drains("logits"), done("logits", b))
                    dve.tensor_reduce(tok(top), tok(logit), AX.X, ALU.max).then_inc(route_dve, 1)
                    dve.wait_ge(route_dve, value(b, 12, 1))
                    dve.tensor_tensor(tok(zed), tok(logit), over_ch(top, EXPERTS), ALU.subtract).then_inc(route_dve, 1)
                    dve.tensor_tensor(tok(equal), tok(logit), over_ch(top, EXPERTS), ALU.is_equal).then_inc(route_dve, 1)
                    dve.wait_ge(route_dve, value(b, 12, 3))
                    dve.tensor_tensor(tok(order), tok(equal), par("rank")[0:LEN, :].rearrange("p (s e) -> p s e", s=SEQS),
                                      ALU.mult).then_inc(route_dve, 1)
                    dve.wait_ge(route_dve, value(b, 12, 4))
                    dve.tensor_reduce(tok(first), tok(order), AX.X, ALU.max).then_inc(route_dve, 1)
                    dve.wait_ge(route_dve, value(b, 12, 5))
                    dve.tensor_tensor(tok(onehot), tok(order), over_ch(first, EXPERTS), ALU.is_equal).then_inc(route_dve, 1)
                    dve.wait_ge(route_act, value(b, 1, 1))
                    dve.tensor_scalar(tok(expd), tok(zth), -1.0, 1.0, ALU.mult, ALU.add).then_inc(route_dve, 1)
                    dve.wait_ge(route_dve, value(b, 12, 7))
                    dve.reciprocal(tok(expr), tok(expd)).then_inc(route_dve, 1)
                    dve.wait_ge(route_dve, value(b, 12, 8))
                    dve.scalar_tensor_tensor(tok(expz), tok(zth), 1.0, tok(expr), ALU.add, ALU.mult).then_inc(route_dve, 1)
                    dve.wait_ge(route_dve, value(b, 12, 9))
                    dve.tensor_reduce(tok(esum), tok(expz), AX.X, ALU.add).then_inc(route_dve, 1)
                    dve.wait_ge(route_dve, value(b, 12, 10))
                    dve.reciprocal(tok(prob), tok(esum)).then_inc(route_dve, 1)
                    dve.wait_ge(route_dve, value(b, 12, 11))
                    dve.tensor_tensor(tok(gate), tok(onehot), over_ch(prob, EXPERTS), ALU.mult).then_inc(route_dve, 1)
                if 24 <= q <= 31:
                    s = q - 24
                    dve.wait_ge(fills(f"down{s}"), done(f"down{s}", b))
                    if s == 0:
                        dve.wait_ge(route_dve, value(b, 12, 12))
                    dve.wait_ge(mixed_ready, value(b, 3 * SEQS, 3 * max(s - 1, 0)))
                    dve.tensor_tensor(tok(sel[s % 2]), ps(f"down{s}")[0:LEN, :].rearrange("t (e c) -> t e c", e=EXPERTS),
                                      gate[0:LEN, s, :].unsqueeze(2).broadcast_to([LEN, EXPERTS, CH]),
                                      ALU.mult).then_inc(drains(f"down{s}"), 1)
                if q == 31:
                    dve.wait_ge(fills("bias"), done("bias", b))
                    dve.tensor_tensor(tok(h4_bias), tok_ps("bias"), tok(h4), ALU.add).then_inc(drains("bias"), 1)

            def read_sums(b):
                dve.wait_ge(prod_summed, value(b, SLOTS, SLOTS))
                dve.wait_ge(h3_ready, value(b, 1, 0))
                dve.tensor_tensor(tok(ysum), ybank[0:LEN, :, :], over_seq("scale"), ALU.mult).then_inc(ysum_ready, 1)

            def products(q, f):
                dve.wait_ge(wsign_ready, value(f, SLOTS, q + 1))
                dve.wait_ge(prod_summed, value(f, SLOTS, q - 1))
                if q % HALF == 0:
                    dve.wait_ge(xsign_ready, value(f, 4, 2 * (q // HALF) + 2))
                dve.tensor_tensor(prod[q % 2][:, :, 0:COLS], wsign[q % 2][:, :, :],
                                  xsign[q // HALF][:, :].unsqueeze(1).broadcast_to([P, 2, COLS]),
                                  ALU.mult).then_inc(prod_ready, 1)

            dve.wait_ge(params_landed, 16)
            dve.tensor_tensor(taps[:, :, :], par("conv_w").rearrange("p (f k) -> p f k", f=TAPS),
                              par("filt").unsqueeze(2).broadcast_to([P, TAPS, CH]), ALU.mult).then_inc(setup_dve, 1)
            dve.tensor_copy(pair_sum[:, :], par("pair_sum")).then_inc(setup_dve, 1)
            dve.wait_ge(setup_act, 3)
            dve.wait_ge(experts_landed, 48)
            dve.tensor_tensor(ew[:, :], ew[:, :], ew_hi[:, :], ALU.subtract).then_inc(setup_dve, 1)
            dve.wait_ge(setup_dve, 3)
            dve.tensor_copy(signs_w[:, :], ew[:, :]).then_inc(setup_dve, 1)
            dve.wait_ge(setup_dve, 4)
            dve.tensor_tensor(signs_w[64:P, :], ew[64:P, :], signs_w[64:P, :], ALU.subtract).then_inc(setup_dve, 1)
            dve.tensor_copy(signs_w[0:32, :], ew_hi[0:32, :]).then_inc(setup_dve, 1)

            def iteration(c, has_a, has_f, has_b):
                for q in range(SLOTS):
                    if has_b and q == 0:
                        read_sums((c, -1))
                    if has_f:
                        products(q, (c, 0))
                    if has_f and q == 0:
                        open_gates(1, (c, 0))
                    if has_a:
                        a_steps(q, (c, 1))
                    if has_b:
                        b_steps(q, (c, -1))

            schedule(dve, iteration)

        @block.gpsimd
        def _(pool):
            def centre(n, chunk, t, src):
                pool.wait_ge(norm_dve[n], value(chunk, 4, 2))
                pool.tensor_tensor(tok(t["xc"]), tok(src), over_ch(t["mean"]), ALU.subtract).then_inc(norm_pool[n], 1)

            def normalise(n, chunk, t):
                pool.wait_ge(norm_dve[n], value(chunk, 4, 4))
                pool.tensor_tensor(tok(t["rstd"]), tok(t["var"]), tok(power), ALU.pow).then_inc(norm_pool[n], 1)
                pool.wait_ge(norm_pool[n], value(chunk, 3, 2))
                pool.tensor_tensor(tok(t["xn"]), tok(t["xc"]), over_ch(t["rstd"]), ALU.mult).then_inc(norm_pool[n], 1)

            def a_steps(q, a):
                if q == 10:
                    centre(1, a, normA, h1)
                    pool.tensor_tensor(tok(h1_by), tok(h1), over_seq("b_y"), ALU.add).then_inc(h1_by_ready, 1)
                if q == 12:
                    normalise(1, a, normA)
                for h in (0, 1):
                    if q == 16 + 4 * h:
                        pool.wait_ge(drains(f"delta{h}"), done(f"delta{h}", a))
                        stand_alone(pool)
                        pool.tensor_scalar(decay[:, :], th[:, :], -0.5, 0.5, ALU.mult, ALU.add).then_inc(decay_ready, 1)
                        pool.wait_ge(decay_ready, value(a, 4, 2 * h + 1))
                        stand_alone(pool)
                        pool.memset(decay[:, :].rearrange("p (s t) -> p s t", t=LEN)[:, :, 0:1], 0.0)\
                            .then_inc(decay_ready, 1)
                if q == 24:
                    centre(2, a, normA, h2)
                if q == 26:
                    normalise(2, a, normA)

            def b_steps(q, b):
                if q == 0:
                    pool.wait_ge(ysum_ready, value(b, 1, 1))
                    pool.wait_ge(h2_parked_ready, value(b, 1, 1))
                    pool.tensor_tensor(tok(h3), tok(ysum), tok(h2_parked), ALU.add).then_inc(h3_ready, 1)
                if q == 1:
                    centre(3, b, normB, h3)
                if q == 3:
                    normalise(3, b, normB)
                if q == 15:
                    centre(4, b, normB, h4)
                if q == 17:
                    normalise(4, b, normB)
                if 24 <= q <= 31:
                    s = q - 24
                    pool.wait_ge(drains(f"down{s}"), done(f"down{s}", b))
                    src = sel[s % 2]
                    pool.tensor_tensor(tok(fold4), src[0:LEN, 0:4, :], src[0:LEN, 4:8, :], ALU.add).then_inc(mixed_ready, 1)
                    pool.wait_ge(mixed_ready, value(b, 3 * SEQS, 3 * s + 1))
                    pool.tensor_tensor(tok(fold2), fold4[0:LEN, 0:2, :], fold4[0:LEN, 2:4, :], ALU.add).then_inc(mixed_ready, 1)
                    pool.wait_ge(mixed_ready, value(b, 3 * SEQS, 3 * s + 2))
                    pool.tensor_tensor(mixed[0:LEN, s, :], fold2[0:LEN, 0, :], fold2[0:LEN, 1, :], ALU.add)\
                        .then_inc(mixed_ready, 1)
                if q == 31:
                    pool.wait_ge(drains("bias"), done("bias", b))
                    pool.wait_ge(mixed_ready, value(b, 3 * SEQS, 3 * SEQS))
                    pool.wait_ge(stored, value(b, 16, 0))
                    pool.tensor_tensor(tok(h5), tok(h4_bias), tok(mixed), ALU.add).then_inc(h5_ready, 1)

            def park(c):
                pool.wait_ge(drains("y"), done("y", c))
                pool.wait_ge(h3_ready, value(c, 1, 0))
                stand_alone(pool)
                pool.tensor_copy(tok(h2_parked), tok(h2)).then_inc(h2_parked_ready, 1)

            pool.memset(ew[:, :], 0.0).then_inc(ew_zeroed, 1)
            pool.memset(power[:, :], -0.5).then_inc(setup_pool, 1)
            for i in (0, 1):
                pool.memset(prod[i][:, :, COLS:ZCOLS], 0.0).then_inc(setup_pool, 1)
            pool.wait_ge(params_landed, 16)
            pool.wait_ge(setup_pool, 3)

            def iteration(c, has_a, has_f, has_b):
                for q in range(SLOTS):
                    if has_a:
                        a_steps(q, (c, 1))
                    if has_b:
                        b_steps(q, (c, -1))
                    if has_f and q == 0:
                        park((c, 0))

            schedule(pool, iteration)


def packed_parameters(w):
    f = {k: np.asarray(v, np.float32) for k, v in w.items()}
    pk = np.zeros((P, PACKED), np.float32)

    def put(name, a, r0=0, c0=0):
        a = np.asarray(a, np.float32)
        pk[r0:r0 + a.shape[0], AT[name][0] + c0:AT[name][0] + c0 + a.shape[1]] = a

    def row(name, v, n=1):
        put(name, np.tile(v.reshape(1, -1), (P, n)))

    def both(name, a):
        put(name, np.tile(a, (2, 1)))

    put("conv_w", f["L0_tok_W_k"].reshape(TAPS, DIM, CH).transpose(1, 0, 2).reshape(DIM, -1))
    put("filt", f["L0_tok_filt"].T)
    row("conv_b", f["L0_tok_b_k"])
    both("w_x", f["L0_attn_Wx"])
    both("w_b", f["L0_attn_Wbc"][:, :STATE])
    both("w_c", f["L0_attn_Wbc"][:, STATE:])
    both("w_delta", f["L0_attn_Wd"])
    put("b_x", f["L0_attn_bx"].reshape(-1, 1))
    put("b_b", f["L0_attn_bbc"][:STATE].reshape(-1, 1))
    put("b_c", f["L0_attn_bbc"][STATE:].reshape(-1, 1))
    put("b_delta", f["L0_attn_bd"].reshape(-1, 1))
    put("w_y", f["L0_attn_Wy"])
    row("b_y", f["L0_attn_by"])
    for part in range(3):
        for h in (0, 1):
            put("w_gate", f["L0_ffn_proj_w"].T, CH * h, 32 * part)
        put("b_gate", f["L0_ffn_proj_b"].reshape(-1, 1), 32 * part)
    row("scale", f["L0_ffn_scale"])
    both("w_enc", np.concatenate([f["L1_attn_kw1"].T, f["L1_attn_qw1"].T], 1))
    put("b_enc", np.concatenate([f["L1_attn_kb1"], f["L1_attn_qb1"]]).reshape(-1, 1))
    for i, n in enumerate("kq"):
        for h in (0, 1):
            for twice in (0, 1):
                put("w_phase", f[f"L1_attn_{n}w2"].T, CH * i, (2 * i + h) * P + CH * h + PHASES * twice)
    put("b_key", np.tile(f["L1_attn_kb2"], 4).reshape(-1, 1))
    put("b_query", np.tile(f["L1_attn_qb2"], 4).reshape(-1, 1))
    both("w_value", f["L1_attn_vw"].T)
    row("b_value", f["L1_attn_vb"])
    both("w_up", f["L1_ffn_W1"])
    put("b_up", f["L1_ffn_b1"].reshape(2, P).T)
    put("w_route", f["L1_ffn_Wg"].reshape(2, P, EXPERTS).transpose(1, 0, 2).reshape(P, -1))
    row("b_route", f["L1_ffn_bg"], SEQS)
    put("w_down", f["L1_ffn_Wd"].reshape(EXPERTS, 2, P, CH).transpose(2, 1, 0, 3).reshape(P, -1))
    for s in range(SEQS):
        put("b_down", f["L1_ffn_bd"], EXPERTS * s, CH * s)
    put("ident", np.eye(P))
    t = np.arange(1, LEN + 1)
    put("causal", np.triu(np.ones((LEN, LEN))) / np.sqrt(t * PHASES)[None, :])
    put("pair_sum", np.repeat(np.eye(2), CH, axis=0))
    cosine = np.arange(P) % CH < PHASES
    put("fold", np.where(cosine, -1.0, 1.0).reshape(-1, 1))
    put("sin_scale", np.where(cosine, -math.pi, math.pi).reshape(-1, 1))
    put("sin_bias", np.where(cosine, math.pi / 2, 0.0).reshape(-1, 1))
    row("rank", np.arange(EXPERTS, 0, -1, dtype=np.float32), SEQS)
    return pk


def kernel(**inputs):
    import concourse.bacc as bacc
    from concourse.bass_utils import run_bass_kernel_spmd

    a = {k: np.asarray(v) for k, v in inputs.items()}
    weight = a["L0_ffn_weight"]
    arrays = {
        "x_dram": np.ascontiguousarray(a["x"].transpose(2, 0, 1)),
        "params_dram": packed_parameters({k: v for k, v in a.items() if k != "x"}),
        "experts_dram": np.ascontiguousarray(weight[0].transpose(0, 2, 1).reshape(EXPERTS, CH * CH)),
    }
    nc = bacc.Bacc("TRN2", target_bir_lowering=False, num_devices=1)
    args = [nc.dram_tensor(n, v.shape, mybir.dt.from_np(v.dtype), kind="ExternalInput").ap() for n, v in arrays.items()]
    out = nc.dram_tensor("out_dram", (LEN, BATCH, CH), F32, kind="ExternalOutput").ap()
    tower(nc, *args, out)
    r = run_bass_kernel_spmd(nc, [arrays], core_ids=[0])
    return np.ascontiguousarray(r.results[0]["out_dram"].transpose(1, 0, 2))
```

```python
import math
from contextlib import ExitStack

import numpy as np

import concourse.bass as bass
from concourse import mybir

F32 = mybir.dt.float32
BF16 = mybir.dt.bfloat16
F32R = mybir.dt.float32r
ALU = mybir.AluOpType
ACT = mybir.ActivationFunctionType
AX = mybir.AxisListType

P = 128
BATCH, FRAMES, DIM = 128, 125, 128
TAPS = 8
LEN = FRAMES - TAPS
CH = 64
STATE = 128
EXPERTS = 8
PHASES = 32
HID = 256
SEQS = 8
CHUNKS = BATCH // SEQS
PAIRS = SEQS // 2
COLS = PAIRS * LEN
OPAIRS = CH // 2
SLOTS = OPAIRS
HALF = SLOTS // 2
ZCOLS = 480
EPS = 1e-5
GATE_AT = 1e-7

SETUP_SPLIT, SETUP_DVE, SETUP_POOL = 5, 10, 3

A_JOBS = ["conv0", "conv1", "turn", "norm10", "norm11", "x0", "delta0", "b0", "c0", "x1", "delta1", "b1", "c1", "y", "norm20", "norm21", "gate0", "gate1"]
B0_JOBS = ["norm30", "enc0", "phase0", "score0", "attend", "norm40", "up00", "up10", "gateT"]
B1_JOBS = ["norm31", "enc1", "value", "phase1", "score1", "norm41", "up01", "up11", "logits"]
D0_JOBS = ["down0", "down2", "down4", "down6"]
D1_JOBS = ["bias", "down1", "down3", "down5", "down7"]
BANK_OF = {j: ("A", A_JOBS.index(j), len(A_JOBS)) for j in A_JOBS}
BANK_OF |= {j: ("B0", B0_JOBS.index(j), len(B0_JOBS)) for j in B0_JOBS}
BANK_OF |= {j: ("B1", B1_JOBS.index(j), len(B1_JOBS)) for j in B1_JOBS}
BANK_OF |= {j: ("D0", D0_JOBS.index(j), len(D0_JOBS)) for j in D0_JOBS}
BANK_OF |= {j: ("D1", D1_JOBS.index(j), len(D1_JOBS)) for j in D1_JOBS}

PACK = [("w_x", STATE), ("w_b", STATE), ("w_c", STATE), ("w_delta", STATE), ("w_gate", P), ("w_enc", P),
        ("w_up", HID), ("w_value", CH), ("w_route", 2 * EXPERTS), ("w_down", 2 * EXPERTS * CH),
        ("conv_w", TAPS * CH), ("filt", TAPS), ("conv_b", 1), ("b_x", 1), ("b_b", 1), ("b_c", 1), ("b_delta", 1),
        ("w_y", CH), ("b_y", CH), ("b_gate", 1), ("scale", CH), ("b_enc", 1), ("w_phase", P), ("b_phase", 1),
        ("b_value", CH), ("b_up", 2), ("b_route", SEQS * EXPERTS), ("b_down", SEQS * CH), ("ident", P),
        ("causal", LEN), ("pair_sum", 2), ("fold", 1), ("sin_scale", 1), ("sin_bias", 1), ("rank", SEQS * EXPERTS)]
AT, _n = {}, 0
for _name, _w in PACK:
    AT[_name] = (_n, _n + _w)
    _n += _w
PACKED = _n
SPLIT = AT["w_down"][1]


def value(chunk, per, k):
    i, off = chunk
    return max(i * per + off * per + k, 0) if isinstance(i, int) else i * per + (off * per + k)


def done(job, chunk):
    _, j, per = BANK_OF[job]
    return value(chunk, per, j + 1)


def before(job, chunk):
    _, j, per = BANK_OF[job]
    return value(chunk, per, j)


def tower(nc, x, params, experts, out):
    with ExitStack() as ctx:
        def sb(name, shape, dt=F32):
            return ctx.enter_context(nc.sbuf_tensor(name, shape, dt))

        def sem(name):
            return ctx.enter_context(nc.semaphore(name))

        prm = sb("prm", [P, PACKED])

        def par(name):
            return prm[:, AT[name][0]:AT[name][1]]

        w_hi = sb("w_hi", [P, SPLIT], F32R)
        w_lo = sb("w_lo", [P, SPLIT], F32R)

        def hi(name):
            return w_hi[:, AT[name][0]:AT[name][1]]

        def lo(name):
            return w_lo[:, AT[name][0]:AT[name][1]]

        taps = sb("taps", [P, TAPS, CH])
        taps_hi = sb("taps_hi", [P, TAPS, CH], F32R)
        taps_lo = sb("taps_lo", [P, TAPS, CH], F32R)
        half_bx = sb("half_bx", [P, 1])
        half_bd = sb("half_bd", [P, 1])
        signs_w = sb("signs_w", [P, OPAIRS * P], BF16)
        after_setup = sb("ew", [P, OPAIRS * P])
        ew = after_setup[:, :]
        after_setup_2 = sb("ew_hi", [P, OPAIRS * P // 2])
        ew_hi = after_setup_2[:, :].bitcast(BF16)
        pair_sum = sb("pair_sum", [P, 2], BF16)
        power = sb("power", [P, SEQS])

        frames = sb("frames", [P, SEQS, FRAMES])
        frames_hi = sb("frames_hi", [P, SEQS, FRAMES], F32R)
        frames_lo = sb("frames_lo", [P, SEQS, FRAMES], F32R)
        odd_taps = sb("odd_taps", [CH, COLS])
        conv_t = sb("conv_t", [P, COLS])
        h1 = sb("h1", [P, SEQS, CH])
        h1_by = sb("h1_by", [P, SEQS, CH])
        h2 = sb("h2", [P, SEQS, CH])
        h2_parked = sb("h2_parked", [P, SEQS, CH])
        ysum = sb("ysum", [P, SEQS, CH])
        h3 = sb("h3", [P, SEQS, CH])
        h4 = sb("h4", [P, SEQS, CH])
        h4_bias = sb("h4_bias", [P, SEQS, CH])
        h5 = sb("h5", [P, SEQS, CH])
        mixed = sb("mixed", [P, SEQS, CH])

        def norm_set(s):
            return {"sum": sb(f"sum_{s}", [P, SEQS]), "mean": sb(f"mean_{s}", [P, SEQS]),
                    "xc": sb(f"xc_{s}", [P, SEQS, CH]), "sq": sb(f"sq_{s}", [P, SEQS, CH]),
                    "ss": sb(f"ss_{s}", [P, SEQS]), "var": sb(f"var_{s}", [P, SEQS]),
                    "rstd": sb(f"rstd_{s}", [P, SEQS]), "xn": sb(f"xn_{s}", [P, SEQS, CH]),
                    "parts": sb(f"parts_{s}", [P, SEQS, 2, CH])}

        normA, normB = norm_set("a"), norm_set("b")
        xt = {n: [sb(f"xt{n}_{h}", [P, COLS], F32R) for h in (0, 1)] for n in (1, 2, 3, 4)}

        xp = sb("xp", [P, COLS])
        th = sb("th", [P, COLS])
        decay = sb("decay", [P, COLS])
        bx = sb("bx", [P, COLS])
        drive = sb("drive", [P, COLS])
        state = sb("state", [P, COLS])
        yscan = sb("yscan", [P, 2, COLS])

        gates = [sb(f"gates{h}", [P, COLS], BF16) for h in (0, 1)]
        xsign = [sb(f"xsign{h}", [P, COLS], BF16) for h in (0, 1)]
        wsign = [sb(f"wsign{i}", [P, 2, COLS], BF16) for i in (0, 1)]
        prod = [sb(f"prod{i}", [P, 2, ZCOLS], BF16) for i in (0, 1)]

        enc = sb("enc", [P, 2, COLS])
        ang, folded = (after_setup_2[:, i * 2 * COLS:(i + 1) * 2 * COLS].rearrange("p (h c) -> p h c", h=2) for i in (0, 1))
        phase = sb("phase", [P, 2, COLS])
        qphase = sb("qphase", [CH, 2, COLS])
        val = sb("val", [P, SEQS, CH])
        score = sb("score", [P, 2, COLS])

        hid = after_setup[:, 0:4 * COLS].rearrange("p (h k c) -> p h k c", h=2, k=2)
        hid_hi = sb("hid_hi", [P, 2, 2, COLS], F32R)
        hid_lo = sb("hid_lo", [P, 2, 2, COLS], F32R)
        logit = sb("logit", [P, SEQS, EXPERTS])
        top = sb("top", [P, SEQS])
        zed = sb("zed", [P, SEQS, EXPERTS])
        equal = sb("equal", [P, SEQS, EXPERTS])
        zth = sb("zth", [P, SEQS, EXPERTS])
        order = sb("order", [P, SEQS, EXPERTS])
        first = sb("first", [P, SEQS])
        onehot = sb("onehot", [P, SEQS, EXPERTS])
        expd = sb("expd", [P, SEQS, EXPERTS])
        expr = sb("expr", [P, SEQS, EXPERTS])
        expz = sb("expz", [P, SEQS, EXPERTS])
        esum = sb("esum", [P, SEQS])
        prob = sb("prob", [P, SEQS])
        gate = sb("gate", [P, SEQS, EXPERTS])
        gate_t = sb("gate_t", [P, LEN])
        sel = [after_setup[:, 4 * COLS + i * EXPERTS * CH:4 * COLS + (i + 1) * EXPERTS * CH].rearrange("p (e c) -> p e c", e=EXPERTS)
               for i in (0, 1)]

        bank = {b: ctx.enter_context(nc.psum_tensor(f"bank{b}", [P, 512], F32)) for b in ("A", "B0", "B1")}
        bank |= {"D0": bank["B0"], "D1": bank["B1"]}
        wbank = [ctx.enter_context(nc.psum_tensor(f"wbank{i}", [P, 2, 512], F32)) for i in (0, 1)]
        ybank = ctx.enter_context(nc.psum_tensor("ybank", [P, SEQS, CH], F32))

        filled = {b: sem(f"bank{b}_filled") for b in bank}
        drained = {b: sem(f"bank{b}_drained") for b in bank}
        params_landed, experts_landed = sem("params_landed"), sem("experts_landed")
        x_landed, stored = sem("x_landed"), sem("stored")
        ew_zeroed, setup_pool, setup_dve, setup_act = sem("ew_zeroed"), sem("setup_pool"), sem("setup_dve"), sem("setup_act")
        frames_hi_ready, frames_lo_ready, odd_ready = sem("frames_hi_ready"), sem("frames_lo_ready"), sem("odd_ready")
        parts_hi_ready = {n: sem(f"parts_hi{n}_ready") for n in (1, 2, 3, 4)}
        parts_lo_ready = {n: sem(f"parts_lo{n}_ready") for n in (1, 2, 3, 4)}
        qphase_ready = sem("qphase_ready")
        hid_hi_ready, hid_lo_ready = sem("hid_hi_ready"), sem("hid_lo_ready")
        h1_by_ready = sem("h1_by_ready")
        norm_dve = {n: sem(f"norm{n}_dve") for n in (1, 2, 3, 4)}
        norm_pool = {n: sem(f"norm{n}_pool") for n in (1, 2, 3, 4)}
        norm_act = {n: sem(f"norm{n}_act") for n in (1, 2, 3, 4)}
        decay_ready, drive_ready, scanned = sem("decay_ready"), sem("drive_ready"), sem("scanned")
        w_filled, wsign_ready, prod_ready, prod_summed = sem("w_filled"), sem("wsign_ready"), sem("prod_ready"), sem("prod_summed")
        xsign_ready, ysum_ready = sem("xsign_ready"), sem("ysum_ready")
        h3_ready, h2_parked_ready = sem("h3_ready"), sem("h2_parked_ready")
        folded_ready, phase_ready = sem("folded_ready"), sem("phase_ready")
        route_dve, route_act = sem("route_dve"), sem("route_act")
        mixed_ready, h5_ready = sem("mixed_ready"), sem("h5_ready")
        waits_passed = sem("waits_passed")

        def stand_alone(eng):
            eng.sem_inc(waits_passed, 1)

        def fills(job):
            return filled[BANK_OF[job][0]]

        def drains(job):
            return drained[BANK_OF[job][0]]

        def ps(job):
            return bank[BANK_OF[job][0]]

        def tok(t):
            return t[0:LEN, :, :] if len(t.shape) == 3 else t[0:LEN, :]

        def tok_ps(job):
            return ps(job)[0:LEN, :].rearrange("p (s c) -> p s c", s=SEQS)

        def conv_ps(job):
            return ps(job)[:, 0:PAIRS * (LEN + 1)].rearrange("p (s t) -> p s t", s=PAIRS)

        def logits_ps():
            return ps("logits")[0:LEN, 0:SEQS * EXPERTS].rearrange("p (s e) -> p s e", s=SEQS)

        def over_ch(col, n=CH):
            return col[0:LEN, :].unsqueeze(2).broadcast_to([LEN, SEQS, n])

        def over_seq(name, n=CH):
            return par(name)[0:LEN, :].unsqueeze(1).broadcast_to([LEN, SEQS, n])

        def rows(h):
            return slice(CH * h, CH * h + CH)

        def cols(p):
            return slice(p * LEN, p * LEN + LEN)

        block = ctx.enter_context(nc.Block())

        def schedule(eng, iteration, last_looped=CHUNKS - 3):
            def peeled(c):
                iteration(c, c < CHUNKS - 1, 0 <= c < CHUNKS, 1 <= c <= CHUNKS, 2 <= c)

            for c in range(-1, 2):
                peeled(c)
            with eng.Fori(2, last_looped + 1) as c:
                iteration(c, True, True, True, True)
            for c in range(last_looped + 1, CHUNKS + 2):
                peeled(c)

        def exists(c, ahead):
            return not isinstance(c, int) or c + ahead < CHUNKS

        @block.sync
        def _(sp):
            sp.dma_start(prm[:, :], params).then_inc(params_landed, 16)
            sp.wait_ge(ew_zeroed, 1)
            for part in range(3):
                sp.dma_start(ew[32 * part:32 * part + EXPERTS, :], experts).then_inc(experts_landed, 16)

            sp.dma_start(frames[:, :, :], x[:, 0:SEQS, :]).then_inc(x_landed, 16)
            sp.wait_ge(frames_hi_ready, 1)
            sp.wait_ge(frames_lo_ready, 1)
            sp.dma_start(frames[:, :, :], x[:, SEQS:2 * SEQS, :]).then_inc(x_landed, 16)

            def iteration(c, has_a, has_f, has_b, has_d):
                if has_d:
                    sp.wait_ge(h5_ready, value((c, -2), 1, 1))
                    sp.dma_start(out[:, bass.ds((c - 2) * SEQS, SEQS), :], h5[0:LEN, :, :]).then_inc(stored, 16)
                if exists(c, 3):
                    sp.wait_ge(frames_hi_ready, value((c, 2), 1, 1))
                    sp.wait_ge(frames_lo_ready, value((c, 2), 1, 1))
                    sp.dma_start(frames[:, :, :], x[:, bass.ds((c + 3) * SEQS, SEQS), :]).then_inc(x_landed, 16)

            schedule(sp, iteration, last_looped=CHUNKS - 4)
            sp.wait_ge(stored, 16 * CHUNKS)

        @block.tensor
        def _(pe):
            def transposes(n, chunk, h, src):
                job = f"norm{n}{h}"
                pe.wait_ge(drains(job), before(job, chunk))
                pe.wait_ge(parts_hi_ready[n], value(chunk, 1, 1))
                pe.wait_ge(parts_lo_ready[n], value(chunk, 1, 1))
                for p in range(PAIRS):
                    mm = pe.transpose(ps(job)[:, cols(p)],
                                      src["parts"][0:LEN, 2 * p + h, :, :].rearrange("t k c -> t (k c)"),
                                      par("ident")[0:LEN, 0:LEN])
                mm.then_inc(fills(job), 1)

            def project(job, chunk, h, name, n, k=0):
                pe.wait_ge(drains(job), before(job, chunk))
                pe.wait_ge(drains(f"norm{n}{h}"), done(f"norm{n}{h}", chunk))
                pe.matmul(ps(job)[:, 0:COLS], hi(name)[:, k * P:k * P + P], xt[n][h][:, :], start=True, stop=False)
                pe.matmul(ps(job)[:, 0:COLS], lo(name)[:, k * P:k * P + P], xt[n][h][:, :],
                          start=False, stop=True).then_inc(fills(job), 1)

            def a_steps(q, a):
                if q in (1, 3):
                    h = q // 2
                    job = f"conv{h}"
                    pe.wait_ge(drains(job), before(job, a))
                    if h == 0:
                        pe.wait_ge(frames_hi_ready, value(a, 1, 1))
                        pe.wait_ge(frames_lo_ready, value(a, 1, 1))
                    parts = ((taps_hi, frames_hi), (taps_hi, frames_lo), (taps_lo, frames_hi))
                    n = 0
                    for f in range(0, TAPS, 2):
                        for tap, frame in parts:
                            mm = pe.matmul(conv_ps(job), tap[:, f:f + 2, :].rearrange("p f k -> p (f k)"),
                                           frame[:, h::2, f:f + LEN + 1], start=(n == 0), stop=(n == 3 * TAPS // 2 - 1))
                            n += 1
                    mm.then_inc(fills(job), 1)
                if q == 5:
                    pe.wait_ge(drains("turn"), before("turn", a))
                    pe.wait_ge(drains("conv1"), done("conv1", a))
                    for p in range(PAIRS):
                        mm = pe.transpose(tok_ps("turn")[:, 2 * p:2 * p + 2, :].rearrange("t s c -> t (s c)"),
                                          conv_t[:, cols(p)], par("ident"))
                    mm.then_inc(fills("turn"), 1)
                if q in (12, 13):
                    transposes(1, a, q - 12, normA)
                for h in (0, 1):
                    for i, w in enumerate(("x", "delta", "b", "c")):
                        if q == 14 + 4 * h + i:
                            project(f"{w}{h}", a, h, f"w_{w}", 1)
                if q == 22:
                    pe.wait_ge(drains("y"), before("y", a))
                    for s in range(SEQS):
                        mm = pe.matmul(tok_ps("y")[:, s, :], yscan[:, s % 2, cols(s // 2)], par("w_y"),
                                       start=True, stop=True)
                    mm.then_inc(fills("y"), 1)
                if q in (29, 30):
                    transposes(2, a, q - 29, normA)
                if q == 31:
                    project("gate0", a, 0, "w_gate", 2)

            def b_steps(q, b):
                if q == 7:
                    pe.wait_ge(drains("down6"), done("down6", (b[0], b[1] - 1)))
                    pe.wait_ge(drains("down7"), done("down7", (b[0], b[1] - 1)))
                    transposes(3, b, 0, normB)
                    transposes(3, b, 1, normB)
                if q == 8:
                    project("enc0", b, 0, "w_enc", 3)
                    project("enc1", b, 1, "w_enc", 3)
                if q == 9:
                    pe.wait_ge(drains("value"), before("value", b))
                    for s in range(SEQS):
                        tokens = xt[3][s % 2][:, cols(s // 2)]
                        pe.matmul(tok_ps("value")[:, s, :], tokens, hi("w_value"), start=True, stop=False)
                        mm = pe.matmul(tok_ps("value")[:, s, :], tokens, lo("w_value"), start=False, stop=True)
                    mm.then_inc(fills("value"), 1)
                if q == 10:
                    for h in (0, 1):
                        job = f"phase{h}"
                        pe.wait_ge(drains(job), before(job, b))
                        pe.wait_ge(drains(f"enc{h}"), done(f"enc{h}", b))
                        pe.matmul(ps(job)[:, 0:COLS], par("w_phase"), enc[:, h, :], start=True, stop=True)\
                          .then_inc(fills(job), 1)
                if q == 14:
                    pe.wait_ge(qphase_ready, value(b, 1, 1))
                    for h in (0, 1):
                        job = f"score{h}"
                        pe.wait_ge(drains(job), before(job, b))
                        for p in range(PAIRS):
                            mm = pe.matmul(ps(job)[0:LEN, cols(p)], phase[0:CH, h, cols(p)], qphase[:, h, cols(p)],
                                           start=True, stop=True)
                        mm.then_inc(fills(job), 1)
                if q == 15:
                    pe.wait_ge(drains("attend"), before("attend", b))
                    pe.wait_ge(drains("value"), done("value", b))
                    pe.wait_ge(drains("score1"), done("score1", b))
                    for s in range(SEQS):
                        mm = pe.matmul(tok_ps("attend")[:, s, :], score[0:LEN, s % 2, cols(s // 2)], val[0:LEN, s, :],
                                       start=True, stop=True)
                    mm.then_inc(fills("attend"), 1)
                if q == 21:
                    transposes(4, b, 0, normB)
                    transposes(4, b, 1, normB)
                for h in (0, 1):
                    if q == 22 + h:
                        for k in (0, 1):
                            project(f"up{h}{k}", b, h, "w_up", 4, k)
                if q in (25, 26):
                    h = q - 25
                    pe.wait_ge(drains("logits"), before("logits", b))
                    pe.wait_ge(hid_hi_ready, value(b, 4, 2 * h + 2))
                    pe.wait_ge(hid_lo_ready, value(b, 4, 2 * h + 2))
                    for s in range(h, SEQS, 2):
                        for k in (0, 1):
                            route = slice(k * EXPERTS, (k + 1) * EXPERTS)
                            tokens_hi, tokens_lo = (t[:, s % 2, k, cols(s // 2)] for t in (hid_hi, hid_lo))
                            pe.matmul(logits_ps()[:, s, :], tokens_hi, hi("w_route")[:, route], start=(k == 0), stop=False)
                            pe.matmul(logits_ps()[:, s, :], tokens_hi, lo("w_route")[:, route], start=False, stop=False)
                            mm = pe.matmul(logits_ps()[:, s, :], tokens_lo, hi("w_route")[:, route],
                                           start=False, stop=(k == 1))
                    if h == 1:
                        mm.then_inc(fills("logits"), 1)
                if q == 31:
                    pe.wait_ge(drains("gateT"), before("gateT", b))
                    pe.wait_ge(route_dve, value(b, 12, 12))
                    stand_alone(pe)
                    pe.transpose(ps("gateT")[0:SEQS * EXPERTS, 0:LEN],
                                 gate[0:LEN, :, :].rearrange("t s e -> t (s e)"),
                                 par("ident")[0:LEN, 0:LEN]).then_inc(fills("gateT"), 1)

            def d_steps(q, d):
                if q == 1:
                    pe.wait_ge(drains("logits"), done("logits", d))
                    pe.wait_ge(drains("bias"), before("bias", d))
                    pe.wait_ge(drains("gateT"), done("gateT", d))
                    pe.matmul(ps("bias")[0:LEN, :], gate_t[0:SEQS * EXPERTS, :], par("b_down")[0:SEQS * EXPERTS, :],
                              start=True, stop=True).then_inc(fills("bias"), 1)
                for s in range(SEQS):
                    if q != min(s + 1, SEQS - 2):
                        continue
                    job = f"down{s}"
                    pe.wait_ge(drains(job), before(job, d))
                    for k in (0, 1):
                        down = slice(k * EXPERTS * CH, (k + 1) * EXPERTS * CH)
                        tokens_hi, tokens_lo = (t[:, s % 2, k, cols(s // 2)] for t in (hid_hi, hid_lo))
                        pe.matmul(ps(job)[0:LEN, :], tokens_hi, hi("w_down")[:, down], start=(k == 0), stop=False)
                        pe.matmul(ps(job)[0:LEN, :], tokens_hi, lo("w_down")[:, down], start=False, stop=False)
                        mm = pe.matmul(ps(job)[0:LEN, :], tokens_lo, hi("w_down")[:, down], start=False, stop=(k == 1))
                    mm.then_inc(fills(job), 1)

            def expert_weights(q, f):
                pe.wait_ge(wsign_ready, value(f, SLOTS, q - 1))
                if q % HALF == 0:
                    pe.wait_ge(drains(f"gate{q // HALF}"), done(f"gate{q // HALF}", f))
                for j in (0, 1):
                    k = 2 * (q % HALF) + j
                    mm = pe.matmul(wbank[q % 2][:, j, 0:COLS], signs_w[:, k * P:(k + 1) * P], gates[q // HALF][:, :],
                                   start=True, stop=True)
                mm.then_inc(w_filled, 1)

            def sum_products(q, f):
                pe.wait_ge(prod_ready, value(f, SLOTS, q + 1))
                if q == 0:
                    pe.wait_ge(ysum_ready, value(f, 1, 0))
                for p in range(PAIRS):
                    for j in (0, 1):
                        o = 2 * (2 * (q % HALF) + j)
                        mm = pe.matmul(ybank[:, 2 * p + q // HALF, o:o + 2], prod[q % 2][:, j, p * LEN:p * LEN + P],
                                       pair_sum[:, :], start=True, stop=True)
                mm.then_inc(prod_summed, 1)

            pe.wait_ge(params_landed, 16)
            pe.wait_ge(setup_dve, SETUP_SPLIT)

            def iteration(c, has_a, has_f, has_b, has_d):
                if has_f:
                    if isinstance(c, int) and c == 0:
                        pe.wait_ge(setup_dve, SETUP_DVE)
                        pe.wait_ge(setup_pool, SETUP_POOL)
                    expert_weights(0, (c, 0))
                    expert_weights(1, (c, 0))
                for q in range(SLOTS):
                    if has_f and 0 < q < SLOTS - 1:
                        expert_weights(q + 1, (c, 0))
                    if has_b and q == 0:
                        sum_products(SLOTS - 1, (c, -1))
                    if has_f and q > 0:
                        sum_products(q - 1, (c, 0))
                    if has_f and q == 0:
                        project("gate1", (c, 0), 1, "w_gate", 2)
                    if has_a:
                        a_steps(q, (c, 1))
                    if has_d:
                        d_steps(q, (c, -2))
                    if has_b:
                        b_steps(q, (c, -1))

            schedule(pe, iteration)

        @block.scalar
        def _(act):
            def turned(n, chunk, h):
                job = f"norm{n}{h}"
                act.wait_ge(fills(job), done(job, chunk))
                act.activation(xt[n][h][:, :], ps(job)[:, 0:COLS], ACT.Copy).then_inc(drains(job), 1)

            def squares(n, chunk, t):
                act.wait_ge(norm_pool[n], value(chunk, 3, 1))
                act.activation(tok(t["sq"]), tok(t["xc"]), ACT.Square).then_inc(norm_act[n], 1)

            def input_signs(h, f):
                act.wait_ge(prod_ready, value(f, SLOTS, HALF * (h + 1) - SLOTS))
                act.wait_ge(drains(f"norm2{h}"), done(f"norm2{h}", f))
                for half in (0, 1):
                    act.activation(xsign[h][rows(half), :], xt[2][h][0:CH, :].bitcast(F32), ACT.Sign).then_inc(xsign_ready, 1)

            def a_steps(q, a):
                if q in (2, 4):
                    h = q // 2 - 1
                    job = f"conv{h}"
                    act.wait_ge(fills(job), done(job, a))
                    if h == 1:
                        act.wait_ge(drains("conv0"), done("conv0", a))
                    act.activation(odd_taps[:, :].rearrange("p (s t) -> p s t", s=PAIRS),
                                   conv_ps(job)[CH:P, :, 1:LEN + 1], ACT.Identity,
                                   bias=par("conv_b")[CH:P, :]).then_inc(odd_ready, 1)
                if q == 6:
                    act.wait_ge(fills("turn"), done("turn", a))
                    act.activation(tok(h1), tok_ps("turn"), ACT.Relu).then_inc(drains("turn"), 1)
                if q == 8:
                    squares(1, a, normA)
                if q in (13, 14):
                    turned(1, a, q - 13)
                for h in (0, 1):
                    if q == 15 + 4 * h:
                        act.wait_ge(fills(f"x{h}"), done(f"x{h}", a))
                        act.activation(xp[:, :], ps(f"x{h}")[:, 0:COLS], ACT.Identity, bias=half_bx[:, 0:1],
                                       scale=0.5).then_inc(drains(f"x{h}"), 1)
                    if q == 16 + 4 * h:
                        act.wait_ge(fills(f"delta{h}"), done(f"delta{h}", a))
                        act.activation(th[:, :], ps(f"delta{h}")[:, 0:COLS], ACT.Tanh, bias=half_bd[:, 0:1],
                                       scale=0.5).then_inc(drains(f"delta{h}"), 1)
                if q == 25:
                    squares(2, a, normA)
                if q in (30, 31):
                    turned(2, a, q - 30)
                if q == 31:
                    input_signs(0, a)

            def b_steps(q, b):
                if q == 3:
                    squares(3, b, normB)
                if q == 8:
                    turned(3, b, 0)
                    turned(3, b, 1)
                if q == 9:
                    for h in (0, 1):
                        act.wait_ge(fills(f"enc{h}"), done(f"enc{h}", b))
                        act.activation(enc[:, h, :], ps(f"enc{h}")[:, 0:COLS], ACT.Tanh,
                                       bias=par("b_enc")).then_inc(drains(f"enc{h}"), 1)
                if q == 11:
                    for h in (0, 1):
                        job = f"phase{h}"
                        act.wait_ge(fills(job), done(job, b))
                        act.activation(ang[:, h, :], ps(job)[:, 0:COLS], ACT.Tanh,
                                       bias=par("b_phase")).then_inc(drains(job), 1)
                if q == 13:
                    act.wait_ge(folded_ready, value(b, 2, 2))
                    act.activation(phase[:, :, :], folded[:, :, :], ACT.Sin, bias=par("sin_bias"),
                                   scale=par("sin_scale")).then_inc(phase_ready, 1)
                if q == 18:
                    squares(4, b, normB)
                if q == 22:
                    turned(4, b, 0)
                    turned(4, b, 1)
                for h in (0, 1):
                    if q == 23 + h:
                        for k in (0, 1):
                            act.wait_ge(fills(f"up{h}{k}"), done(f"up{h}{k}", b))
                            act.activation(hid[:, h, k, :], ps(f"up{h}{k}")[:, 0:COLS], ACT.Gelu,
                                           bias=par("b_up")[:, k:k + 1]).then_inc(drains(f"up{h}{k}"), 1)
                if q == 29:
                    act.wait_ge(route_dve, value(b, 12, 2))
                    act.activation(tok(zth), tok(zed), ACT.Tanh, scale=0.5).then_inc(route_act, 1)

            def d_steps(q, d):
                if q == 0:
                    act.wait_ge(fills("gateT"), done("gateT", d))
                    act.activation(gate_t[0:SEQS * EXPERTS, :], ps("gateT")[0:SEQS * EXPERTS, 0:LEN],
                                   ACT.Copy).then_inc(drains("gateT"), 1)

            def weight_signs(q, f):
                act.wait_ge(w_filled, value(f, SLOTS, q + 1))
                act.wait_ge(prod_ready, value(f, SLOTS, q - 1))
                act.activation(wsign[q % 2][:, :, :], wbank[q % 2][:, :, 0:COLS], ACT.Sign).then_inc(wsign_ready, 1)

            act.wait_ge(params_landed, 16)
            act.mul(half_bx[:, :], par("b_x"), 0.5).then_inc(setup_act, 1)
            act.mul(half_bd[:, :], par("b_delta"), 0.5).then_inc(setup_act, 1)
            act.wait_ge(experts_landed, 48)
            act.activation(ew_hi, ew[:, :], ACT.Copy).then_inc(setup_act, 1)
            act.wait_ge(setup_act, 3)

            def iteration(c, has_a, has_f, has_b, has_d):
                for q in range(SLOTS):
                    if has_f and q == 0:
                        input_signs(1, (c, 0))
                    if has_f:
                        weight_signs(q, (c, 0))
                    if has_a:
                        a_steps(q, (c, 1))
                    if has_d:
                        d_steps(q, (c, -2))
                    if has_b:
                        b_steps(q, (c, -1))

            schedule(act, iteration)

        @block.vector
        def _(dve):
            def sums(n, chunk, t, src):
                dve.tensor_reduce(tok(t["sum"]), tok(src), AX.X, ALU.add).then_inc(norm_dve[n], 1)
                dve.wait_ge(norm_dve[n], value(chunk, 4, 1))
                dve.tensor_scalar(tok(t["mean"]), tok(t["sum"]), 1.0 / CH, None, ALU.mult).then_inc(norm_dve[n], 1)

            def variances(n, chunk, t):
                dve.wait_ge(norm_act[n], value(chunk, 1, 1))
                dve.tensor_reduce(tok(t["ss"]), tok(t["sq"]), AX.X, ALU.add).then_inc(norm_dve[n], 1)
                dve.wait_ge(norm_dve[n], value(chunk, 4, 3))
                dve.tensor_scalar(tok(t["var"]), tok(t["ss"]), 1.0 / CH, EPS, ALU.mult, ALU.add).then_inc(norm_dve[n], 1)

            def high_part(n, chunk, t):
                dve.wait_ge(norm_pool[n], value(chunk, 3, 3))
                dve.tensor_copy(t["parts"][0:LEN, :, 0, :].bitcast(F32R), tok(t["xn"])).then_inc(parts_hi_ready[n], 1)

            def split_frames(a):
                dve.wait_ge(x_landed, value(a, 16, 16))
                dve.wait_ge(fills("conv1"), done("conv1", (a[0], a[1] - 1)))
                dve.tensor_copy(frames_hi[:, :, :], frames[:, :, :]).then_inc(frames_hi_ready, 1)

            def open_gates(h, a):
                dve.wait_ge(fills(f"gate{h}"), done(f"gate{h}", a))
                dve.tensor_scalar(gates[h][:, :], ps(f"gate{h}")[:, 0:COLS], par("b_gate"), GATE_AT,
                                  ALU.add, ALU.is_gt).then_inc(drains(f"gate{h}"), 1)

            def a_steps(q, a):
                if q in (2, 4):
                    h = q // 2 - 1
                    job = f"conv{h}"
                    dve.wait_ge(odd_ready, value(a, 2, h + 1))
                    dve.tensor_tensor(conv_t[rows(h), :].rearrange("p (s t) -> p s t", s=PAIRS),
                                      conv_ps(job)[0:CH, :, 0:LEN],
                                      odd_taps[:, :].rearrange("p (s t) -> p s t", s=PAIRS), ALU.add)\
                       .then_inc(drains(job), 1)
                if q == 6:
                    dve.wait_ge(drains("turn"), done("turn", a))
                    sums(1, a, normA, h1)
                if q == 9:
                    variances(1, a, normA)
                if q == 11:
                    high_part(1, a, normA)
                for h in (0, 1):
                    if q == 17 + 4 * h:
                        dve.wait_ge(fills(f"b{h}"), done(f"b{h}", a))
                        dve.wait_ge(drains(f"delta{h}"), done(f"delta{h}", a))
                        dve.scalar_tensor_tensor(bx[:, :], ps(f"b{h}")[:, 0:COLS], par("b_b"), xp[:, :],
                                                 ALU.add, ALU.mult).then_inc(drains(f"b{h}"), 1)
                        dve.wait_ge(drains(f"b{h}"), done(f"b{h}", a))
                        dve.scalar_tensor_tensor(drive[:, :], th[:, :], 1.0, bx[:, :],
                                                 ALU.add, ALU.mult).then_inc(drive_ready, 1)
                        dve.wait_ge(drive_ready, value(a, 2, h + 1))
                        dve.wait_ge(decay_ready, value(a, 4, 2 * h + 2))
                        dve.tensor_tensor_scan(state[:, :], decay[:, :], drive[:, :], 0.0,
                                               ALU.mult, ALU.add).then_inc(scanned, 1)
                    if q == 18 + 4 * h:
                        dve.wait_ge(fills(f"c{h}"), done(f"c{h}", a))
                        dve.wait_ge(scanned, value(a, 2, h + 1))
                        dve.scalar_tensor_tensor(yscan[:, h, :], ps(f"c{h}")[:, 0:COLS], par("b_c"), state[:, :],
                                                 ALU.add, ALU.mult).then_inc(drains(f"c{h}"), 1)
                if q == 23:
                    dve.wait_ge(fills("y"), done("y", a))
                    dve.wait_ge(h1_by_ready, value(a, 1, 1))
                    dve.tensor_tensor(tok(h2), tok_ps("y"), tok(h1_by), ALU.add).then_inc(drains("y"), 1)
                    dve.wait_ge(drains("y"), done("y", a))
                    sums(2, a, normA, h2)
                if q == 26:
                    variances(2, a, normA)
                if q == 28:
                    high_part(2, a, normA)

            def b_steps(q, b):
                if q == 0:
                    dve.wait_ge(prod_summed, value(b, SLOTS, SLOTS))
                    dve.tensor_tensor(tok(ysum), ybank[0:LEN, :, :], over_seq("scale"), ALU.mult).then_inc(ysum_ready, 1)
                    dve.wait_ge(ysum_ready, value(b, 1, 1))
                    dve.wait_ge(h2_parked_ready, value(b, 1, 1))
                    dve.tensor_tensor(tok(h3), tok(ysum), tok(h2_parked), ALU.add).then_inc(h3_ready, 1)
                if q == 1:
                    dve.wait_ge(h3_ready, value(b, 1, 1))
                    sums(3, b, normB, h3)
                if q == 4:
                    variances(3, b, normB)
                if q == 6:
                    high_part(3, b, normB)
                if q == 10:
                    dve.wait_ge(fills("value"), done("value", b))
                    dve.tensor_tensor(tok(val), tok_ps("value"), over_seq("b_value"), ALU.add).then_inc(drains("value"), 1)
                if q == 12:
                    for h in (0, 1):
                        dve.wait_ge(drains(f"phase{h}"), done(f"phase{h}", b))
                        dve.scalar_tensor_tensor(folded[:, h, :], ang[:, h, :], par("fold"), ang[:, h, :],
                                                 ALU.mult, ALU.max).then_inc(folded_ready, 1)
                if q == 13:
                    dve.wait_ge(phase_ready, value(b, 1, 1))
                    dve.tensor_copy(qphase[:, :, :], phase[CH:P, :, :]).then_inc(qphase_ready, 1)
                if q == 15:
                    for h in (0, 1):
                        dve.wait_ge(fills(f"score{h}"), done(f"score{h}", b))
                        dve.tensor_tensor(score[0:LEN, h, :].rearrange("t (p s) -> t p s", p=PAIRS),
                                          ps(f"score{h}")[0:LEN, 0:COLS].rearrange("t (p s) -> t p s", p=PAIRS),
                                          par("causal")[0:LEN, :].unsqueeze(1).broadcast_to([LEN, PAIRS, LEN]),
                                          ALU.mult).then_inc(drains(f"score{h}"), 1)
                if q == 16:
                    dve.wait_ge(fills("attend"), done("attend", b))
                    dve.tensor_tensor(tok(h4), tok_ps("attend"), tok(h3), ALU.add).then_inc(drains("attend"), 1)
                    dve.wait_ge(drains("attend"), done("attend", b))
                    sums(4, b, normB, h4)
                if q == 18:
                    variances(4, b, normB)
                if q == 20:
                    high_part(4, b, normB)
                for h in (0, 1):
                    if q == 24 + h:
                        for k in (0, 1):
                            dve.wait_ge(drains(f"up{h}{k}"), done(f"up{h}{k}", b))
                            dve.tensor_copy(hid_hi[:, h, k, :], hid[:, h, k, :]).then_inc(hid_hi_ready, 1)
                if q == 28:
                    dve.wait_ge(fills("logits"), done("logits", b))
                    dve.tensor_tensor(tok(logit), logits_ps(), par("b_route")[0:LEN, :].rearrange("p (s e) -> p s e", s=SEQS),
                                      ALU.add).then_inc(drains("logits"), 1)
                    dve.wait_ge(drains("logits"), done("logits", b))
                    dve.tensor_reduce(tok(top), tok(logit), AX.X, ALU.max).then_inc(route_dve, 1)
                    dve.wait_ge(route_dve, value(b, 12, 1))
                    dve.tensor_tensor(tok(zed), tok(logit), over_ch(top, EXPERTS), ALU.subtract).then_inc(route_dve, 1)
                    dve.tensor_tensor(tok(equal), tok(logit), over_ch(top, EXPERTS), ALU.is_equal).then_inc(route_dve, 1)
                    dve.wait_ge(route_dve, value(b, 12, 3))
                    dve.tensor_tensor(tok(order), tok(equal), par("rank")[0:LEN, :].rearrange("p (s e) -> p s e", s=SEQS),
                                      ALU.mult).then_inc(route_dve, 1)
                    dve.wait_ge(route_dve, value(b, 12, 4))
                    dve.tensor_reduce(tok(first), tok(order), AX.X, ALU.max).then_inc(route_dve, 1)
                    dve.wait_ge(route_dve, value(b, 12, 5))
                    dve.tensor_tensor(tok(onehot), tok(order), over_ch(first, EXPERTS), ALU.is_equal).then_inc(route_dve, 1)
                if q == 30:
                    dve.wait_ge(route_act, value(b, 1, 1))
                    dve.tensor_scalar(tok(expd), tok(zth), -1.0, 1.0, ALU.mult, ALU.add).then_inc(route_dve, 1)
                    dve.wait_ge(route_dve, value(b, 12, 7))
                    dve.reciprocal(tok(expr), tok(expd)).then_inc(route_dve, 1)
                    dve.wait_ge(route_dve, value(b, 12, 8))
                    dve.scalar_tensor_tensor(tok(expz), tok(zth), 1.0, tok(expr), ALU.add, ALU.mult).then_inc(route_dve, 1)
                    dve.wait_ge(route_dve, value(b, 12, 9))
                    dve.tensor_reduce(tok(esum), tok(expz), AX.X, ALU.add).then_inc(route_dve, 1)
                    dve.wait_ge(route_dve, value(b, 12, 10))
                    dve.reciprocal(tok(prob), tok(esum)).then_inc(route_dve, 1)
                    dve.wait_ge(route_dve, value(b, 12, 11))
                    dve.tensor_tensor(tok(gate), tok(onehot), over_ch(prob, EXPERTS), ALU.mult).then_inc(route_dve, 1)

            def d_steps(q, d):
                if q == 2:
                    dve.wait_ge(fills("bias"), done("bias", d))
                    dve.tensor_tensor(tok(h4_bias), tok_ps("bias"), tok(h4), ALU.add).then_inc(drains("bias"), 1)
                for s in range(SEQS):
                    if q != min(s + 2, SEQS - 1):
                        continue
                    dve.wait_ge(fills(f"down{s}"), done(f"down{s}", d))
                    dve.tensor_tensor(tok(sel[s % 2]), ps(f"down{s}")[0:LEN, :].rearrange("t (e c) -> t e c", e=EXPERTS),
                                      gate[0:LEN, s, :].unsqueeze(2).broadcast_to([LEN, EXPERTS, CH]),
                                      ALU.mult).then_inc(drains(f"down{s}"), 1)
                    dve.wait_ge(drains(f"down{s}"), done(f"down{s}", d))
                    dve.wait_ge(h5_ready, value(d, 1, 0))
                    dve.tensor_reduce(mixed[0:LEN, s, :], tok(sel[s % 2]).rearrange("t e c -> t c e"),
                                      AX.X, ALU.add).then_inc(mixed_ready, 1)

            def products(q, f):
                dve.wait_ge(wsign_ready, value(f, SLOTS, q + 1))
                dve.wait_ge(prod_summed, value(f, SLOTS, q - 1))
                if q % HALF == 0:
                    dve.wait_ge(xsign_ready, value(f, 4, 2 * (q // HALF) + 2))
                dve.tensor_tensor(prod[q % 2][:, :, 0:COLS], wsign[q % 2][:, :, :],
                                  xsign[q // HALF][:, :].unsqueeze(1).broadcast_to([P, 2, COLS]),
                                  ALU.mult).then_inc(prod_ready, 1)

            dve.wait_ge(params_landed, 16)
            dve.tensor_copy(w_hi[:, :], prm[:, 0:SPLIT]).then_inc(setup_dve, 1)
            dve.tensor_tensor(taps[:, :, :], par("conv_w").rearrange("p (f k) -> p f k", f=TAPS),
                              par("filt").unsqueeze(2).broadcast_to([P, TAPS, CH]), ALU.mult).then_inc(setup_dve, 1)
            dve.wait_ge(setup_dve, 2)
            dve.tensor_copy(taps_hi[:, :, :], taps[:, :, :]).then_inc(setup_dve, 1)
            dve.tensor_tensor(w_lo[:, :], prm[:, 0:SPLIT], w_hi[:, :].bitcast(F32), ALU.subtract).then_inc(setup_dve, 1)
            dve.wait_ge(setup_dve, 3)
            dve.tensor_tensor(taps_lo[:, :, :], taps[:, :, :], taps_hi[:, :, :].bitcast(F32),
                              ALU.subtract).then_inc(setup_dve, 1)
            dve.tensor_copy(pair_sum[:, :], par("pair_sum")).then_inc(setup_dve, 1)
            dve.wait_ge(setup_act, 3)
            dve.wait_ge(experts_landed, 48)
            dve.tensor_tensor(ew[:, :], ew[:, :], ew_hi, ALU.subtract).then_inc(setup_dve, 1)
            dve.wait_ge(setup_dve, 7)
            dve.tensor_copy(signs_w[:, :], ew[:, :]).then_inc(setup_dve, 1)
            dve.wait_ge(setup_dve, 8)
            dve.tensor_tensor(signs_w[64:P, :], ew[64:P, :], signs_w[64:P, :], ALU.subtract).then_inc(setup_dve, 1)
            dve.tensor_copy(signs_w[0:32, :], ew_hi[0:32, :]).then_inc(setup_dve, 1)

            split_frames((0, 0))

            def iteration(c, has_a, has_f, has_b, has_d):
                for q in range(SLOTS):
                    if has_f:
                        products(q, (c, 0))
                    if has_b:
                        b_steps(q, (c, -1))
                    if has_f and q == 0:
                        open_gates(1, (c, 0))
                    if has_f and q == 1:
                        dve.tensor_copy(tok(h2_parked), tok(h2)).then_inc(h2_parked_ready, 1)
                    if q == 14 and exists(c, 2):
                        split_frames((c, 2))
                    if has_a:
                        a_steps(q, (c, 1))
                    if has_d:
                        d_steps(q, (c, -2))
                if has_a:
                    open_gates(0, (c, 1))

            schedule(dve, iteration)

        @block.gpsimd
        def _(pool):
            def centre(n, chunk, t, src):
                pool.wait_ge(norm_dve[n], value(chunk, 4, 2))
                pool.tensor_tensor(tok(t["xc"]), tok(src), over_ch(t["mean"]), ALU.subtract).then_inc(norm_pool[n], 1)

            def normalise(n, chunk, t):
                pool.wait_ge(norm_dve[n], value(chunk, 4, 4))
                pool.tensor_tensor(tok(t["rstd"]), tok(t["var"]), tok(power), ALU.pow).then_inc(norm_pool[n], 1)
                pool.wait_ge(norm_pool[n], value(chunk, 3, 2))
                pool.tensor_tensor(tok(t["xn"]), tok(t["xc"]), over_ch(t["rstd"]), ALU.mult).then_inc(norm_pool[n], 1)

            def low_part(n, chunk, t):
                pool.wait_ge(parts_hi_ready[n], value(chunk, 1, 1))
                pool.wait_ge(norm_pool[n], value(chunk, 3, 3))
                pool.tensor_tensor(t["parts"][0:LEN, :, 1, :], tok(t["xn"]), t["parts"][0:LEN, :, 0, :],
                                   ALU.subtract).then_inc(parts_lo_ready[n], 1)

            def split_frames(a):
                pool.wait_ge(frames_hi_ready, value(a, 1, 1))
                pool.tensor_tensor(frames_lo[:, :, :], frames[:, :, :], frames_hi[:, :, :].bitcast(F32),
                                   ALU.subtract).then_inc(frames_lo_ready, 1)

            def a_steps(q, a):
                if q == 6:
                    centre(1, a, normA, h1)
                    pool.tensor_tensor(tok(h1_by), tok(h1), over_seq("b_y"), ALU.add).then_inc(h1_by_ready, 1)
                if q == 9:
                    normalise(1, a, normA)
                if q == 11:
                    low_part(1, a, normA)
                for h in (0, 1):
                    if q == 16 + 4 * h:
                        pool.wait_ge(drains(f"delta{h}"), done(f"delta{h}", a))
                        stand_alone(pool)
                        pool.tensor_scalar(decay[:, :], th[:, :], -0.5, 0.5, ALU.mult, ALU.add).then_inc(decay_ready, 1)
                        pool.wait_ge(decay_ready, value(a, 4, 2 * h + 1))
                        stand_alone(pool)
                        pool.memset(decay[:, :].rearrange("p (s t) -> p s t", t=LEN)[:, :, 0:1], 0.0)\
                            .then_inc(decay_ready, 1)
                if q == 23:
                    centre(2, a, normA, h2)
                if q == 26:
                    normalise(2, a, normA)
                if q == 28:
                    low_part(2, a, normA)

            def b_steps(q, b):
                if q == 1:
                    centre(3, b, normB, h3)
                if q == 4:
                    normalise(3, b, normB)
                    low_part(3, b, normB)
                if q == 16:
                    centre(4, b, normB, h4)
                if q == 18:
                    normalise(4, b, normB)
                    low_part(4, b, normB)
                for h in (0, 1):
                    if q == 24 + h:
                        for k in (0, 1):
                            pool.wait_ge(hid_hi_ready, value(b, 4, 2 * h + k + 1))
                            pool.tensor_tensor(hid_lo[:, h, k, :], hid[:, h, k, :], hid_hi[:, h, k, :].bitcast(F32),
                                               ALU.subtract).then_inc(hid_lo_ready, 1)

            def d_steps(q, d):
                if q == 8:
                    pool.wait_ge(drains("bias"), done("bias", d))
                    pool.wait_ge(mixed_ready, value(d, SEQS, SEQS))
                    pool.wait_ge(stored, value(d, 16, 0))
                    pool.tensor_tensor(tok(h5), tok(h4_bias), tok(mixed), ALU.add).then_inc(h5_ready, 1)

            pool.memset(ew[:, :], 0.0).then_inc(ew_zeroed, 1)
            pool.memset(power[:, :], -0.5).then_inc(setup_pool, 1)
            for i in (0, 1):
                pool.memset(prod[i][:, :, COLS:ZCOLS], 0.0).then_inc(setup_pool, 1)
            pool.wait_ge(params_landed, 16)
            pool.wait_ge(setup_pool, 3)

            split_frames((0, 0))

            def iteration(c, has_a, has_f, has_b, has_d):
                for q in range(SLOTS):
                    if q == 14 and exists(c, 2):
                        split_frames((c, 2))
                    if has_a:
                        a_steps(q, (c, 1))
                    if has_d:
                        d_steps(q, (c, -2))
                    if has_b:
                        b_steps(q, (c, -1))

            schedule(pool, iteration)


def packed_parameters(w):
    f = {k: np.asarray(v, np.float32) for k, v in w.items()}
    pk = np.zeros((P, PACKED), np.float32)

    def put(name, a, r0=0, c0=0):
        a = np.asarray(a, np.float32)
        pk[r0:r0 + a.shape[0], AT[name][0] + c0:AT[name][0] + c0 + a.shape[1]] = a

    def row(name, v, n=1):
        put(name, np.tile(v.reshape(1, -1), (P, n)))

    def both(name, a):
        put(name, np.tile(a, (2, 1)))

    put("conv_w", f["L0_tok_W_k"].reshape(TAPS, DIM, CH).transpose(1, 0, 2).reshape(DIM, -1))
    put("filt", f["L0_tok_filt"].T)
    both("conv_b", f["L0_tok_b_k"].reshape(-1, 1))
    both("w_x", f["L0_attn_Wx"])
    both("w_b", f["L0_attn_Wbc"][:, :STATE])
    both("w_c", f["L0_attn_Wbc"][:, STATE:])
    both("w_delta", f["L0_attn_Wd"])
    put("b_x", f["L0_attn_bx"].reshape(-1, 1))
    put("b_b", f["L0_attn_bbc"][:STATE].reshape(-1, 1))
    put("b_c", f["L0_attn_bbc"][STATE:].reshape(-1, 1))
    put("b_delta", f["L0_attn_bd"].reshape(-1, 1))
    put("w_y", f["L0_attn_Wy"])
    row("b_y", f["L0_attn_by"])
    for part in range(3):
        for h in (0, 1):
            put("w_gate", f["L0_ffn_proj_w"].T, CH * h, 32 * part)
        put("b_gate", f["L0_ffn_proj_b"].reshape(-1, 1), 32 * part)
    row("scale", f["L0_ffn_scale"])
    both("w_enc", np.concatenate([f["L1_attn_kw1"].T, f["L1_attn_qw1"].T], 1))
    put("b_enc", np.concatenate([f["L1_attn_kb1"], f["L1_attn_qb1"]]).reshape(-1, 1))
    for i, n in enumerate("kq"):
        for twice in (0, 1):
            put("w_phase", f[f"L1_attn_{n}w2"].T, CH * i, CH * i + PHASES * twice)
            put("b_phase", f[f"L1_attn_{n}b2"].reshape(-1, 1), CH * i + PHASES * twice)
    both("w_value", f["L1_attn_vw"].T)
    row("b_value", f["L1_attn_vb"])
    both("w_up", f["L1_ffn_W1"])
    put("b_up", f["L1_ffn_b1"].reshape(2, P).T)
    put("w_route", f["L1_ffn_Wg"].reshape(2, P, EXPERTS).transpose(1, 0, 2).reshape(P, -1))
    row("b_route", f["L1_ffn_bg"], SEQS)
    put("w_down", f["L1_ffn_Wd"].reshape(EXPERTS, 2, P, CH).transpose(2, 1, 0, 3).reshape(P, -1))
    for s in range(SEQS):
        put("b_down", f["L1_ffn_bd"], EXPERTS * s, CH * s)
    put("ident", np.eye(P))
    t = np.arange(1, LEN + 1)
    put("causal", np.triu(np.ones((LEN, LEN))) / np.sqrt(t * PHASES)[None, :])
    put("pair_sum", np.repeat(np.eye(2), CH, axis=0))
    cosine = np.arange(P) % CH < PHASES
    put("fold", np.where(cosine, -1.0, 1.0).reshape(-1, 1))
    put("sin_scale", np.where(cosine, -math.pi, math.pi).reshape(-1, 1))
    put("sin_bias", np.where(cosine, math.pi / 2, 0.0).reshape(-1, 1))
    row("rank", np.arange(EXPERTS, 0, -1, dtype=np.float32), SEQS)
    return pk


def kernel(**inputs):
    import concourse.bacc as bacc
    from concourse.bass_utils import run_bass_kernel_spmd

    a = {k: np.asarray(v) for k, v in inputs.items()}
    weight = a["L0_ffn_weight"]
    arrays = {
        "x_dram": np.ascontiguousarray(a["x"].transpose(2, 0, 1)),
        "params_dram": packed_parameters({k: v for k, v in a.items() if k != "x"}),
        "experts_dram": np.ascontiguousarray(weight[0].transpose(0, 2, 1).reshape(EXPERTS, CH * CH)),
    }
    nc = bacc.Bacc("TRN2", target_bir_lowering=False, num_devices=1)
    args = [nc.dram_tensor(n, v.shape, mybir.dt.from_np(v.dtype), kind="ExternalInput").ap() for n, v in arrays.items()]
    out = nc.dram_tensor("out_dram", (LEN, BATCH, CH), F32, kind="ExternalOutput").ap()
    tower(nc, *args, out)
    r = run_bass_kernel_spmd(nc, [arrays], core_ids=[0])
    return np.ascontiguousarray(r.results[0]["out_dram"].transpose(1, 0, 2))
```

```python
import math
from contextlib import ExitStack

import numpy as np

import concourse.bass as bass
from concourse import mybir

F32 = mybir.dt.float32
BF16 = mybir.dt.bfloat16
F32R = mybir.dt.float32r
ALU = mybir.AluOpType
ACT = mybir.ActivationFunctionType
AX = mybir.AxisListType

P = 128
BATCH, FRAMES, DIM = 128, 125, 128
TAPS = 8
LEN = FRAMES - TAPS
CH = 64
STATE = 128
EXPERTS = 8
PHASES = 32
HID = 256
SEQS = 8
CHUNKS = BATCH // SEQS
PAIRS = SEQS // 2
COLS = PAIRS * LEN
OPAIRS = CH // 2
SLOTS = OPAIRS
HALF = SLOTS // 2
ZCOLS = 480
EPS = 1e-5
GATE_AT = 1e-7

SETUP_TAPS, SETUP_SPLIT, SETUP_DVE, SETUP_POOL = 3, 7, 12, 3

C_JOBS = ["conv0", "conv1", "turn"]
A_JOBS = ["norm10", "norm11", "delta0", "x0", "b0", "c0", "delta1", "x1", "b1", "c1", "y", "norm20", "norm21", "gate0", "gate1"]
B0_JOBS = ["norm30", "enc0", "phase0", "score0", "attend", "norm40", "up00", "up10"]
B1_JOBS = ["norm31", "enc1", "value", "phase1", "score1", "norm41", "up01", "up11", "logits"]
D0_JOBS = ["down0", "down2", "down4", "down6", "bias"]
D1_JOBS = ["down1", "gateT", "down3", "down5", "down7"]
BANK_OF = {j: ("A", A_JOBS.index(j), len(A_JOBS)) for j in A_JOBS}
BANK_OF |= {j: ("C", C_JOBS.index(j), len(C_JOBS)) for j in C_JOBS}
BANK_OF |= {j: ("B0", B0_JOBS.index(j), len(B0_JOBS)) for j in B0_JOBS}
BANK_OF |= {j: ("B1", B1_JOBS.index(j), len(B1_JOBS)) for j in B1_JOBS}
BANK_OF |= {j: ("D0", D0_JOBS.index(j), len(D0_JOBS)) for j in D0_JOBS}
BANK_OF |= {j: ("D1", D1_JOBS.index(j), len(D1_JOBS)) for j in D1_JOBS}

PE_AT = dict(down0=0.5, down1=1.0, down2=1.5, gateT=2, down3=3.5, down4=4.0, norm10=4, down5=4.5, down6=5.0,
             down7=6.0, bias=6.5, norm11=6.5, delta0=7.5, norm30=8.0, norm31=8, x0=8.5, b0=8.5, enc1=9.5,
             enc0=10, c0=10, value=10.0, phase0=11, phase1=11, delta1=11.0, x1=13, b1=13.5, c1=14.0,
             score0=15.0, score1=15.0, attend0=16, attend1=16, y=16.5, conv0=18.5, conv1=19.5, norm41=20.5,
             turn=21.0, norm40=21.5, up0=23.0, norm20=24.5, up1=24.5, norm21=25.0, logits0=26.0, logits1=27.0,
             gate0=27.5, gate1=30.0)
ACT_AT = dict(squares1=2.0, gateT=3.0, squares3=3.0, norm10=5, signs1=6, norm11=7.0, delta0=8.5, norm30=9,
              x0=9.5, norm31=9.5, enc1=10.0, enc0=11.0, phase0=12, phase1=12.0, delta1=12.5, x1=14.5, sin=14.5,
              squares4=18.5, conv0=19.0, squares2=20.0, conv1=20.5, turn=21.0, norm40=22, norm41=23.0,
              up0=23.5, norm20=25, up1=25.5, signs0=26.5, norm21=27.0, route=30.5)
DVE_AT = dict(ysum=0, sums1=0.5, sums3=0.5, down0=1.0, down1=2.0, variances1=2.0, down2=2.5, down3=4.0,
              high1=4, variances3=4.0, down4=4.5, park=5.5, down5=5.5, down6=5.5, high3=6.5, bias=6.5,
              down7=7.0, scan0=9, b0=9, c0=10.0, value=10, frames=11.5, phase0=12.0, phase1=12.0, scan1=14,
              b1=14, queries=14.5, c1=15.5, score0=16, score1=16.0, attend=16.5, y=17, variances4=17.0,
              conv0=19.0, high4=20.0, variances2=20.5, conv1=20.5, high2=21.5, up0=23.5, up1=25.5, logits=28.5,
              gate0=29.0, prob=30.0)
POOL_AT = dict(centre1=1.0, centre3=3.5, normalise1=4, low1=5.5, normalise3=6.0, low3=9.5, h5=10.5,
               delta0=12.0, delta1=12.5, frames=15.0, centre4=16.0, normalise4=16.5, centre2=17, low4=18.5,
               normalise2=19.0, low2=19.5, up0=20.5, up1=20.5)

PACK = [("conv_w", TAPS * CH), ("filt", TAPS), ("conv_b", 1), ("ident", P),
        ("w_x", STATE), ("w_b", STATE), ("w_c", STATE), ("w_delta", STATE), ("w_gate", P), ("w_enc", P),
        ("w_up", HID), ("w_value", CH), ("w_route", 2 * EXPERTS), ("w_down", 2 * EXPERTS * CH),
        ("b_x", 1), ("b_b", 1), ("b_c", 1), ("b_delta", 1),
        ("w_y", CH), ("b_y", CH), ("b_gate", 1), ("scale", CH), ("b_enc", 1), ("w_phase", P), ("b_phase", 1),
        ("b_value", CH), ("b_up", 2), ("b_route", SEQS * EXPERTS), ("b_down", SEQS * CH),
        ("causal", LEN), ("pair_sum", 2), ("fold", 1), ("sin_scale", 1), ("sin_bias", 1), ("rank", SEQS * EXPERTS)]
AT, _n = {}, 0
for _name, _w in PACK:
    AT[_name] = (_n, _n + _w)
    _n += _w
PACKED = _n
CONV_PARAMS = AT["ident"][1]
SPLIT = AT["w_x"][0], AT["w_down"][1]


def value(chunk, per, k):
    i, off = chunk
    return max(i * per + off * per + k, 0) if isinstance(i, int) else i * per + (off * per + k)


def chunk_before(chunk):
    return chunk[0], chunk[1] - 1


def chunk_after(chunk):
    return chunk[0], chunk[1] + 1


def done(job, chunk):
    _, j, per = BANK_OF[job]
    return value(chunk, per, j + 1)


def before(job, chunk):
    _, j, per = BANK_OF[job]
    return value(chunk, per, j)


def tower(nc, x, params, experts, out):
    with ExitStack() as ctx:
        def sb(name, shape, dt=F32):
            return ctx.enter_context(nc.sbuf_tensor(name, shape, dt))

        def sem(name):
            return ctx.enter_context(nc.semaphore(name))

        prm = sb("prm", [P, PACKED])

        def par(name):
            return prm[:, AT[name][0]:AT[name][1]]

        w_hi = sb("w_hi", [P, SPLIT[1] - SPLIT[0]], F32R)
        w_lo = sb("w_lo", [P, SPLIT[1] - SPLIT[0]], F32R)
        route_w = sb("route_w", [P, 2, 2 * EXPERTS], F32R)

        def hi(name):
            return w_hi[:, AT[name][0] - SPLIT[0]:AT[name][1] - SPLIT[0]]

        def lo(name):
            return w_lo[:, AT[name][0] - SPLIT[0]:AT[name][1] - SPLIT[0]]

        taps = sb("taps", [P, TAPS, CH])
        taps_hi = sb("taps_hi", [P, TAPS, CH], F32R)
        taps_lo = sb("taps_lo", [P, TAPS, CH], F32R)
        half_bx = sb("half_bx", [P, 1])
        half_bd = sb("half_bd", [P, 1])
        signs_w = sb("signs_w", [P, OPAIRS * P], BF16)
        after_setup = sb("ew", [P, OPAIRS * P])
        ew = after_setup[:, :]
        after_setup_2 = sb("ew_hi", [P, OPAIRS * P // 2])
        ew_hi = after_setup_2[:, :].bitcast(BF16)
        pair_sum = sb("pair_sum", [P, 2], BF16)
        power = sb("power", [P, SEQS])

        frames = sb("frames", [P, SEQS, FRAMES])
        frames_hi = sb("frames_hi", [P, SEQS, FRAMES], F32R)
        frames_lo = sb("frames_lo", [P, SEQS, FRAMES], F32R)
        odd_taps = sb("odd_taps", [CH, COLS])
        conv_t = sb("conv_t", [P, COLS])
        h1 = sb("h1", [P, SEQS, CH])
        h1_by = sb("h1_by", [P, SEQS, CH])
        h2 = sb("h2", [P, SEQS, CH])
        h2_parked = sb("h2_parked", [P, SEQS, CH])
        ysum = sb("ysum", [P, SEQS, CH])
        h3 = sb("h3", [P, SEQS, CH])
        h4 = sb("h4", [P, SEQS, CH])
        h4_bias = sb("h4_bias", [P, SEQS, CH])
        h5 = sb("h5", [P, SEQS, CH])
        mixed = sb("mixed", [P, SEQS, CH])

        def norm_set(s):
            return {"sum": sb(f"sum_{s}", [P, SEQS]), "mean": sb(f"mean_{s}", [P, SEQS]),
                    "xc": sb(f"xc_{s}", [P, SEQS, CH]), "sq": sb(f"sq_{s}", [P, SEQS, CH]),
                    "ss": sb(f"ss_{s}", [P, SEQS]), "var": sb(f"var_{s}", [P, SEQS]),
                    "rstd": sb(f"rstd_{s}", [P, SEQS]), "xn": sb(f"xn_{s}", [P, SEQS, CH]),
                    "parts": sb(f"parts_{s}", [P, SEQS, 2, CH])}

        normA, normB = norm_set("a"), norm_set("b")
        xt = {n: [sb(f"xt{n}_{h}", [P, COLS], F32R) for h in (0, 1)] for n in (1, 2, 3, 4)}

        xp = sb("xp", [P, COLS])
        th = sb("th", [P, COLS])
        decay = sb("decay", [P, COLS])
        bx = sb("bx", [P, COLS])
        drive = sb("drive", [P, COLS])
        state = sb("state", [P, COLS])
        yscan = sb("yscan", [P, 2, COLS])

        gates = [sb(f"gates{h}", [P, COLS], BF16) for h in (0, 1)]
        xsign = [sb(f"xsign{h}", [P, COLS], BF16) for h in (0, 1)]
        wsign = [sb(f"wsign{i}", [P, 2, COLS], BF16) for i in (0, 1)]
        prod = [sb(f"prod{i}", [P, 2, ZCOLS], BF16) for i in (0, 1)]

        enc = sb("enc", [P, 2, COLS])
        ang, folded = (after_setup_2[:, i * 2 * COLS:(i + 1) * 2 * COLS].rearrange("p (h c) -> p h c", h=2) for i in (0, 1))
        phase = sb("phase", [P, 2, COLS])
        qphase = sb("qphase", [CH, 2, COLS])
        val = sb("val", [P, SEQS, CH])
        score = sb("score", [P, 2, COLS])

        hid = after_setup[:, 0:4 * COLS].rearrange("p (h k c) -> p h k c", h=2, k=2)
        hid_hi = sb("hid_hi", [P, 2, 2, COLS], F32R)
        hid_lo = sb("hid_lo", [P, 2, 2, COLS], F32R)
        logit_hi = sb("logit_hi", [P, SEQS, EXPERTS])
        logit = sb("logit", [P, SEQS, EXPERTS])
        top = sb("top", [P, SEQS])
        zed = sb("zed", [P, SEQS, EXPERTS])
        equal = sb("equal", [P, SEQS, EXPERTS])
        zth = sb("zth", [P, SEQS, EXPERTS])
        order = sb("order", [P, SEQS, EXPERTS])
        first = sb("first", [P, SEQS])
        onehot = sb("onehot", [P, SEQS, EXPERTS])
        expd = sb("expd", [P, SEQS, EXPERTS])
        expr = sb("expr", [P, SEQS, EXPERTS])
        expz = sb("expz", [P, SEQS, EXPERTS])
        esum = sb("esum", [P, SEQS])
        prob = sb("prob", [P, SEQS])
        gate = sb("gate", [P, SEQS, EXPERTS])
        gate_t = sb("gate_t", [P, LEN])
        sel = [after_setup[:, 4 * COLS + i * EXPERTS * CH:4 * COLS + (i + 1) * EXPERTS * CH].rearrange("p (e c) -> p e c", e=EXPERTS)
               for i in (0, 1)]

        bank = {b: ctx.enter_context(nc.psum_tensor(f"bank{b}", [P, 512], F32)) for b in ("A", "B0", "B1")}
        bank |= {"C": bank["A"], "D0": bank["B0"], "D1": bank["B1"]}
        wbank = [ctx.enter_context(nc.psum_tensor(f"wbank{i}", [P, 2, 512], F32)) for i in (0, 1)]
        ybank = ctx.enter_context(nc.psum_tensor("ybank", [P, SEQS, CH], F32))

        filled = {b: sem(f"bank{b}_filled") for b in bank}
        drained = {b: sem(f"bank{b}_drained") for b in bank}
        conv_params_landed, params_landed, experts_landed = sem("conv_params_landed"), sem("params_landed"), sem("experts_landed")
        x_landed, stored = sem("x_landed"), sem("stored")
        ew_zeroed, setup_pool, setup_dve, setup_act = sem("ew_zeroed"), sem("setup_pool"), sem("setup_dve"), sem("setup_act")
        frames_hi_ready, frames_lo_ready, odd_ready = sem("frames_hi_ready"), sem("frames_lo_ready"), sem("odd_ready")
        parts_hi_ready = {n: sem(f"parts_hi{n}_ready") for n in (1, 2, 3, 4)}
        parts_lo_ready = {n: sem(f"parts_lo{n}_ready") for n in (1, 2, 3, 4)}
        qphase_ready = sem("qphase_ready")
        hid_hi_ready, hid_lo_ready = sem("hid_hi_ready"), sem("hid_lo_ready")
        h1_by_ready = sem("h1_by_ready")
        norm_dve = {n: sem(f"norm{n}_dve") for n in (1, 2, 3, 4)}
        norm_pool = {n: sem(f"norm{n}_pool") for n in (1, 2, 3, 4)}
        norm_act = {n: sem(f"norm{n}_act") for n in (1, 2, 3, 4)}
        decay_ready, drive_ready, scanned = sem("decay_ready"), sem("drive_ready"), sem("scanned")
        w_filled, wsign_ready, prod_ready, prod_summed = sem("w_filled"), sem("wsign_ready"), sem("prod_ready"), sem("prod_summed")
        xsign_ready, ysum_ready = sem("xsign_ready"), sem("ysum_ready")
        h3_ready, h2_parked_ready = sem("h3_ready"), sem("h2_parked_ready")
        folded_ready, phase_ready = sem("folded_ready"), sem("phase_ready")
        logit_hi_ready = sem("logit_hi_ready")
        route_dve, route_act = sem("route_dve"), sem("route_act")
        mixed_ready, h5_ready = sem("mixed_ready"), sem("h5_ready")
        waits_passed = sem("waits_passed")

        def stand_alone(eng):
            eng.sem_inc(waits_passed, 1)

        def fills(job):
            return filled[BANK_OF[job][0]]

        def drains(job):
            return drained[BANK_OF[job][0]]

        def ps(job):
            return bank[BANK_OF[job][0]]

        def tok(t):
            return t[0:LEN, :, :] if len(t.shape) == 3 else t[0:LEN, :]

        def tok_ps(job):
            return ps(job)[0:LEN, :].rearrange("p (s c) -> p s c", s=SEQS)

        def conv_ps(job):
            return ps(job)[:, 0:PAIRS * (LEN + 1)].rearrange("p (s t) -> p s t", s=PAIRS)

        def logits_ps():
            return ps("logits")[0:LEN, 0:SEQS * 2 * EXPERTS].rearrange("p (s e) -> p s e", s=SEQS)

        def over_ch(col, n=CH):
            return col[0:LEN, :].unsqueeze(2).broadcast_to([LEN, SEQS, n])

        def over_seq(name, n=CH):
            return par(name)[0:LEN, :].unsqueeze(1).broadcast_to([LEN, SEQS, n])

        def rows(h):
            return slice(CH * h, CH * h + CH)

        def cols(p):
            return slice(p * LEN, p * LEN + LEN)

        block = ctx.enter_context(nc.Block())

        def schedule(eng, iteration, last_looped=CHUNKS - 3):
            def peeled(c):
                iteration(c, c < CHUNKS - 2, -1 <= c < CHUNKS - 1, 0 <= c < CHUNKS, 1 <= c <= CHUNKS, 2 <= c)

            for c in range(-2, 3):
                peeled(c)
            with eng.Fori(3, last_looped + 1) as c:
                iteration(c, True, True, True, True, True)
            for c in range(last_looped + 1, CHUNKS + 2):
                peeled(c)

        def exists(c, ahead):
            return not isinstance(c, int) or c + ahead < CHUNKS

        @block.sync
        def _(sp):
            sp.dma_start(prm[:, 0:CONV_PARAMS], params[:, 0:CONV_PARAMS]).then_inc(conv_params_landed, 16)
            sp.dma_start(frames[:, :, :], x[:, 0:SEQS, :]).then_inc(x_landed, 16)
            sp.dma_start(prm[:, CONV_PARAMS:PACKED], params[:, CONV_PARAMS:PACKED]).then_inc(params_landed, 16)
            sp.wait_ge(ew_zeroed, 1)
            for part in range(3):
                sp.dma_start(ew[32 * part:32 * part + EXPERTS, :], experts).then_inc(experts_landed, 16)


            def iteration(c, has_c, has_a, has_f, has_b, has_d):
                if has_d:
                    sp.wait_ge(h5_ready, value((c, -2), 1, 1))
                    sp.dma_start(out[:, bass.ds((c - 2) * SEQS, SEQS), :], h5[0:LEN, :, :]).then_inc(stored, 16)
                if exists(c, 3):
                    sp.wait_ge(frames_hi_ready, value((c, 2), 1, 1))
                    sp.wait_ge(frames_lo_ready, value((c, 2), 1, 1))
                    sp.dma_start(frames[:, :, :], x[:, bass.ds((c + 3) * SEQS, SEQS), :]).then_inc(x_landed, 16)

            schedule(sp, iteration, last_looped=CHUNKS - 4)
            sp.wait_ge(stored, 16 * CHUNKS)

        @block.tensor
        def _(pe):
            def transposes(n, chunk, h, src):
                job = f"norm{n}{h}"
                pe.wait_ge(drains(job), before(job, chunk))
                pe.wait_ge(parts_hi_ready[n], value(chunk, 1, 1))
                pe.wait_ge(parts_lo_ready[n], value(chunk, 1, 1))
                for p in range(PAIRS):
                    mm = pe.transpose(ps(job)[:, cols(p)],
                                      src["parts"][0:LEN, 2 * p + h, :, :].rearrange("t k c -> t (k c)"),
                                      par("ident")[0:LEN, 0:LEN])
                mm.then_inc(fills(job), 1)

            def project(job, chunk, h, name, n, k=0):
                pe.wait_ge(drains(job), before(job, chunk))
                pe.wait_ge(drains(f"norm{n}{h}"), done(f"norm{n}{h}", chunk))
                pe.matmul(ps(job)[:, 0:COLS], hi(name)[:, k * P:k * P + P], xt[n][h][:, :], start=True, stop=False)
                pe.matmul(ps(job)[:, 0:COLS], lo(name)[:, k * P:k * P + P], xt[n][h][:, :],
                          start=False, stop=True).then_inc(fills(job), 1)

            def a_steps(q, a):
                for h in (0, 1):
                    if q == PE_AT[f"norm1{h}"]:
                        transposes(1, a, h, normA)
                for h in (0, 1):
                    for w in ("delta", "x", "b", "c"):
                        if q == PE_AT[f"{w}{h}"]:
                            project(f"{w}{h}", a, h, f"w_{w}", 1)
                if q == PE_AT["y"]:
                    pe.wait_ge(drains("y"), before("y", a))
                    for s in range(SEQS):
                        mm = pe.matmul(tok_ps("y")[:, s, :], yscan[:, s % 2, cols(s // 2)], par("w_y"),
                                       start=True, stop=True)
                    mm.then_inc(fills("y"), 1)
                if q == PE_AT["norm20"] and exists(*chunk_after(a)):
                    pe.wait_ge(drains("turn"), done("turn", chunk_after(a)))
                for h in (0, 1):
                    if q == PE_AT[f"norm2{h}"]:
                        transposes(2, a, h, normA)
                for h in (0, 1):
                    if q == PE_AT[f"gate{h}"]:
                        project(f"gate{h}", a, h, "w_gate", 2)

            def c_steps(q, k):
                for h in (0, 1):
                    if q != PE_AT[f"conv{h}"]:
                        continue
                    job = f"conv{h}"
                    pe.wait_ge(drains(job), before(job, k))
                    if h == 0:
                        pe.wait_ge(drains("y"), done("y", chunk_before(k)))
                        pe.wait_ge(frames_hi_ready, value(k, 1, 1))
                        pe.wait_ge(frames_lo_ready, value(k, 1, 1))
                    parts = ((taps_hi, frames_hi), (taps_hi, frames_lo), (taps_lo, frames_hi))
                    n = 0
                    for f in range(0, TAPS, 2):
                        for tap, frame in parts:
                            mm = pe.matmul(conv_ps(job), tap[:, f:f + 2, :].rearrange("p f k -> p (f k)"),
                                           frame[:, h::2, f:f + LEN + 1], start=(n == 0), stop=(n == 3 * TAPS // 2 - 1))
                            n += 1
                    mm.then_inc(fills(job), 1)
                if q == PE_AT["turn"]:
                    pe.wait_ge(drains("turn"), before("turn", k))
                    for p in range(PAIRS):
                        mm = pe.transpose(tok_ps("turn")[:, 2 * p:2 * p + 2, :].rearrange("t s c -> t (s c)"),
                                          conv_t[:, cols(p)], par("ident"))
                    mm.then_inc(fills("turn"), 1)

            def b_steps(q, b):
                for h, last in enumerate(("bias", "down7")):
                    if q == PE_AT[f"norm3{h}"]:
                        pe.wait_ge(drains(last), done(last, chunk_before(b)))
                        transposes(3, b, h, normB)
                for h in (0, 1):
                    if q == PE_AT[f"enc{h}"]:
                        project(f"enc{h}", b, h, "w_enc", 3)
                if q == PE_AT["value"]:
                    pe.wait_ge(drains("value"), before("value", b))
                    for s in range(SEQS):
                        tokens = xt[3][s % 2][:, cols(s // 2)]
                        pe.matmul(tok_ps("value")[:, s, :], tokens, hi("w_value"), start=True, stop=False)
                        mm = pe.matmul(tok_ps("value")[:, s, :], tokens, lo("w_value"), start=False, stop=True)
                    mm.then_inc(fills("value"), 1)
                for h in (0, 1):
                    if q == PE_AT[f"phase{h}"]:
                        job = f"phase{h}"
                        pe.wait_ge(drains(job), before(job, b))
                        pe.wait_ge(drains(f"enc{h}"), done(f"enc{h}", b))
                        pe.matmul(ps(job)[:, 0:COLS], par("w_phase"), enc[:, h, :], start=True, stop=True)\
                          .then_inc(fills(job), 1)
                for h in (0, 1):
                    if q == PE_AT[f"score{h}"]:
                        pe.wait_ge(qphase_ready, value(b, 1, 1))
                        job = f"score{h}"
                        pe.wait_ge(drains(job), before(job, b))
                        for p in range(PAIRS):
                            mm = pe.matmul(ps(job)[0:LEN, cols(p)], phase[0:CH, h, cols(p)], qphase[:, h, cols(p)],
                                           start=True, stop=True)
                        mm.then_inc(fills(job), 1)
                for h in (0, 1):
                    if q != PE_AT[f"attend{h}"]:
                        continue
                    pe.wait_ge(drains("attend"), before("attend", b))
                    pe.wait_ge(drains("value"), done("value", b))
                    pe.wait_ge(drains(f"score{h}"), done(f"score{h}", b))
                    for s in range(h, SEQS, 2):
                        mm = pe.matmul(tok_ps("attend")[:, s, :], score[0:LEN, s % 2, cols(s // 2)], val[0:LEN, s, :],
                                       start=True, stop=True)
                    if h == 1:
                        mm.then_inc(fills("attend"), 1)
                for h in (0, 1):
                    if q == PE_AT[f"norm4{h}"]:
                        transposes(4, b, h, normB)
                for h in (0, 1):
                    if q == PE_AT[f"up{h}"]:
                        for k in (0, 1):
                            project(f"up{h}{k}", b, h, "w_up", 4, k)
                for h in (0, 1):
                    if q != PE_AT[f"logits{h}"]:
                        continue
                    pe.wait_ge(drains("logits"), before("logits", b))
                    pe.wait_ge(hid_hi_ready, value(b, 4, 2 * h + 2))
                    pe.wait_ge(hid_lo_ready, value(b, 4, 2 * h + 2))
                    for s in range(h, SEQS, 2):
                        for k in (0, 1):
                            tokens_hi, tokens_lo = (t[:, s % 2, k, cols(s // 2)] for t in (hid_hi, hid_lo))
                            pe.matmul(logits_ps()[:, s, :], tokens_hi, route_w[:, k, :], start=(k == 0), stop=False)
                            mm = pe.matmul(logits_ps()[:, s, :], tokens_lo, route_w[:, k, :], start=False, stop=(k == 1))
                    if h == 1:
                        mm.then_inc(fills("logits"), 1)

            def d_steps(q, d):
                for s in range(SEQS):
                    if q != PE_AT[f"down{s}"]:
                        continue
                    job = f"down{s}"
                    if s < 2:
                        last = ("up10", "logits")[s]
                        pe.wait_ge(drains(last), done(last, d))
                    pe.wait_ge(drains(job), before(job, d))
                    for k in (0, 1):
                        down = slice(k * EXPERTS * CH, (k + 1) * EXPERTS * CH)
                        tokens_hi, tokens_lo = (t[:, s % 2, k, cols(s // 2)] for t in (hid_hi, hid_lo))
                        pe.matmul(ps(job)[0:LEN, :], tokens_hi, hi("w_down")[:, down], start=(k == 0), stop=False)
                        pe.matmul(ps(job)[0:LEN, :], tokens_hi, lo("w_down")[:, down], start=False, stop=False)
                        mm = pe.matmul(ps(job)[0:LEN, :], tokens_lo, hi("w_down")[:, down], start=False, stop=(k == 1))
                    mm.then_inc(fills(job), 1)
                if q == PE_AT["gateT"]:
                    pe.wait_ge(drains("gateT"), before("gateT", d))
                    pe.wait_ge(route_dve, value(d, 12, 12))
                    stand_alone(pe)
                    pe.transpose(ps("gateT")[0:SEQS * EXPERTS, 0:LEN],
                                 gate[0:LEN, :, :].rearrange("t s e -> t (s e)"),
                                 par("ident")[0:LEN, 0:LEN]).then_inc(fills("gateT"), 1)
                if q == PE_AT["bias"]:
                    pe.wait_ge(drains("bias"), before("bias", d))
                    pe.wait_ge(drains("gateT"), done("gateT", d))
                    pe.matmul(ps("bias")[0:LEN, :], gate_t[0:SEQS * EXPERTS, :], par("b_down")[0:SEQS * EXPERTS, :],
                              start=True, stop=True).then_inc(fills("bias"), 1)

            def expert_weights(q, f):
                pe.wait_ge(wsign_ready, value(f, SLOTS, q - 1))
                if q % HALF == 0:
                    pe.wait_ge(drains(f"gate{q // HALF}"), done(f"gate{q // HALF}", f))
                for j in (0, 1):
                    k = 2 * (q % HALF) + j
                    mm = pe.matmul(wbank[q % 2][:, j, 0:COLS], signs_w[:, k * P:(k + 1) * P], gates[q // HALF][:, :],
                                   start=True, stop=True)
                mm.then_inc(w_filled, 1)

            def sum_products(q, f):
                pe.wait_ge(prod_ready, value(f, SLOTS, q + 1))
                if q == 0:
                    pe.wait_ge(ysum_ready, value(f, 1, 0))
                for p in range(PAIRS):
                    for j in (0, 1):
                        o = 2 * (2 * (q % HALF) + j)
                        mm = pe.matmul(ybank[:, 2 * p + q // HALF, o:o + 2], prod[q % 2][:, j, p * LEN:p * LEN + P],
                                       pair_sum[:, :], start=True, stop=True)
                mm.then_inc(prod_summed, 1)

            pe.wait_ge(conv_params_landed, 16)
            pe.wait_ge(setup_dve, SETUP_TAPS)

            def iteration(c, has_c, has_a, has_f, has_b, has_d):
                if isinstance(c, int) and c == -1:
                    pe.wait_ge(params_landed, 16)
                    pe.wait_ge(setup_dve, SETUP_SPLIT)
                if has_f:
                    if isinstance(c, int) and c == 0:
                        pe.wait_ge(setup_dve, SETUP_DVE)
                        pe.wait_ge(setup_pool, SETUP_POOL)
                    expert_weights(0, (c, 0))
                    expert_weights(1, (c, 0))
                for q in range(SLOTS):
                    if has_f and 0 < q < SLOTS - 1:
                        expert_weights(q + 1, (c, 0))
                    if has_b and q == 0:
                        sum_products(SLOTS - 1, (c, -1))
                    if has_f and q > 0:
                        sum_products(q - 1, (c, 0))
                    for at in (q, q + 0.5):
                        if has_d:
                            d_steps(at, (c, -2))
                        if has_b:
                            b_steps(at, (c, -1))
                        if has_a:
                            a_steps(at, (c, 1))
                        if has_c:
                            c_steps(at, (c, 2))

            schedule(pe, iteration)

        @block.scalar
        def _(act):
            def turned(n, chunk, h):
                job = f"norm{n}{h}"
                act.wait_ge(fills(job), done(job, chunk))
                act.activation(xt[n][h][:, :], ps(job)[:, 0:COLS], ACT.Copy).then_inc(drains(job), 1)

            def squares(n, chunk, t):
                act.wait_ge(norm_pool[n], value(chunk, 3, 1))
                act.activation(tok(t["sq"]), tok(t["xc"]), ACT.Square).then_inc(norm_act[n], 1)

            def input_signs(h, f):
                act.wait_ge(prod_ready, value(f, SLOTS, HALF * (h + 1) - SLOTS))
                act.wait_ge(drains(f"norm2{h}"), done(f"norm2{h}", f))
                for half in (0, 1):
                    act.activation(xsign[h][rows(half), :], xt[2][h][0:CH, :].bitcast(F32), ACT.Sign).then_inc(xsign_ready, 1)

            def a_steps(q, a):
                if q == ACT_AT["squares1"]:
                    squares(1, a, normA)
                for h in (0, 1):
                    if q == ACT_AT[f"norm1{h}"]:
                        turned(1, a, h)
                    if q == ACT_AT[f"delta{h}"]:
                        act.wait_ge(fills(f"delta{h}"), done(f"delta{h}", a))
                        act.activation(th[:, :], ps(f"delta{h}")[:, 0:COLS], ACT.Tanh, bias=half_bd[:, 0:1],
                                       scale=0.5).then_inc(drains(f"delta{h}"), 1)
                    if q == ACT_AT[f"x{h}"]:
                        act.wait_ge(fills(f"x{h}"), done(f"x{h}", a))
                        act.activation(xp[:, :], ps(f"x{h}")[:, 0:COLS], ACT.Identity, bias=half_bx[:, 0:1],
                                       scale=0.5).then_inc(drains(f"x{h}"), 1)
                if q == ACT_AT["squares2"]:
                    squares(2, a, normA)
                for h in (0, 1):
                    if q == ACT_AT[f"norm2{h}"]:
                        turned(2, a, h)
                if q == ACT_AT["signs0"]:
                    input_signs(0, a)

            def c_steps(q, k):
                for h in (0, 1):
                    if q != ACT_AT[f"conv{h}"]:
                        continue
                    job = f"conv{h}"
                    act.wait_ge(fills(job), done(job, k))
                    if h == 1:
                        act.wait_ge(drains("conv0"), done("conv0", k))
                    act.activation(odd_taps[:, :].rearrange("p (s t) -> p s t", s=PAIRS),
                                   conv_ps(job)[CH:P, :, 1:LEN + 1], ACT.Identity,
                                   bias=par("conv_b")[CH:P, :]).then_inc(odd_ready, 1)
                if q == ACT_AT["turn"]:
                    act.wait_ge(fills("turn"), done("turn", k))
                    act.activation(tok(h1), tok_ps("turn"), ACT.Relu).then_inc(drains("turn"), 1)

            def b_steps(q, b):
                if q == ACT_AT["squares3"]:
                    squares(3, b, normB)
                for h in (0, 1):
                    if q == ACT_AT[f"norm3{h}"]:
                        turned(3, b, h)
                for h in (0, 1):
                    if q == ACT_AT[f"enc{h}"]:
                        act.wait_ge(fills(f"enc{h}"), done(f"enc{h}", b))
                        act.activation(enc[:, h, :], ps(f"enc{h}")[:, 0:COLS], ACT.Tanh,
                                       bias=par("b_enc")).then_inc(drains(f"enc{h}"), 1)
                for h in (0, 1):
                    if q == ACT_AT[f"phase{h}"]:
                        job = f"phase{h}"
                        act.wait_ge(fills(job), done(job, b))
                        act.activation(ang[:, h, :], ps(job)[:, 0:COLS], ACT.Tanh,
                                       bias=par("b_phase")).then_inc(drains(job), 1)
                if q == ACT_AT["sin"]:
                    act.wait_ge(folded_ready, value(b, 2, 2))
                    act.activation(phase[:, :, :], folded[:, :, :], ACT.Sin, bias=par("sin_bias"),
                                   scale=par("sin_scale")).then_inc(phase_ready, 1)
                if q == ACT_AT["squares4"]:
                    squares(4, b, normB)
                for h in (0, 1):
                    if q == ACT_AT[f"norm4{h}"]:
                        turned(4, b, h)
                for h in (0, 1):
                    if q == ACT_AT[f"up{h}"]:
                        for k in (0, 1):
                            act.wait_ge(fills(f"up{h}{k}"), done(f"up{h}{k}", b))
                            act.activation(hid[:, h, k, :], ps(f"up{h}{k}")[:, 0:COLS], ACT.Gelu,
                                           bias=par("b_up")[:, k:k + 1]).then_inc(drains(f"up{h}{k}"), 1)
                if q == ACT_AT["route"]:
                    act.wait_ge(route_dve, value(b, 12, 2))
                    act.activation(tok(zth), tok(zed), ACT.Tanh, scale=0.5).then_inc(route_act, 1)

            def d_steps(q, d):
                if q == ACT_AT["gateT"]:
                    act.wait_ge(fills("gateT"), done("gateT", d))
                    act.activation(gate_t[0:SEQS * EXPERTS, :], ps("gateT")[0:SEQS * EXPERTS, 0:LEN],
                                   ACT.Copy).then_inc(drains("gateT"), 1)

            def weight_signs(q, f):
                act.wait_ge(w_filled, value(f, SLOTS, q + 1))
                act.wait_ge(prod_ready, value(f, SLOTS, q - 1))
                act.activation(wsign[q % 2][:, :, :], wbank[q % 2][:, :, 0:COLS], ACT.Sign).then_inc(wsign_ready, 1)

            act.wait_ge(conv_params_landed, 16)
            act.wait_ge(params_landed, 16)
            act.mul(half_bx[:, :], par("b_x"), 0.5).then_inc(setup_act, 1)
            act.mul(half_bd[:, :], par("b_delta"), 0.5).then_inc(setup_act, 1)
            act.wait_ge(experts_landed, 48)
            act.activation(ew_hi, ew[:, :], ACT.Copy).then_inc(setup_act, 1)
            act.wait_ge(setup_act, 3)

            def iteration(c, has_c, has_a, has_f, has_b, has_d):
                for q in range(SLOTS):
                    if has_f:
                        weight_signs(q, (c, 0))
                    if has_f and q == ACT_AT["signs1"]:
                        input_signs(1, (c, 0))
                    for at in (q, q + 0.5):
                        if has_a:
                            a_steps(at, (c, 1))
                        if has_c:
                            c_steps(at, (c, 2))
                        if has_d:
                            d_steps(at, (c, -2))
                        if has_b:
                            b_steps(at, (c, -1))
            schedule(act, iteration)

        @block.vector
        def _(dve):
            def sums(n, chunk, t, src):
                dve.tensor_reduce(tok(t["sum"]), tok(src), AX.X, ALU.add).then_inc(norm_dve[n], 1)
                dve.wait_ge(norm_dve[n], value(chunk, 4, 1))
                dve.tensor_scalar(tok(t["mean"]), tok(t["sum"]), 1.0 / CH, None, ALU.mult).then_inc(norm_dve[n], 1)

            def variances(n, chunk, t):
                dve.wait_ge(norm_act[n], value(chunk, 1, 1))
                dve.tensor_reduce(tok(t["ss"]), tok(t["sq"]), AX.X, ALU.add).then_inc(norm_dve[n], 1)
                dve.wait_ge(norm_dve[n], value(chunk, 4, 3))
                dve.tensor_scalar(tok(t["var"]), tok(t["ss"]), 1.0 / CH, EPS, ALU.mult, ALU.add).then_inc(norm_dve[n], 1)

            def high_part(n, chunk, t):
                dve.wait_ge(norm_pool[n], value(chunk, 3, 3))
                dve.tensor_copy(t["parts"][0:LEN, :, 0, :].bitcast(F32R), tok(t["xn"])).then_inc(parts_hi_ready[n], 1)

            def split_frames(a):
                dve.wait_ge(x_landed, value(a, 16, 16))
                dve.wait_ge(fills("conv1"), done("conv1", chunk_before(a)))
                dve.tensor_copy(frames_hi[:, :, :], frames[:, :, :]).then_inc(frames_hi_ready, 1)

            def open_gates(h, a):
                dve.wait_ge(fills(f"gate{h}"), done(f"gate{h}", a))
                dve.wait_ge(w_filled, value(a, SLOTS, HALF * (h + 1) - SLOTS))
                dve.tensor_scalar(gates[h][:, :], ps(f"gate{h}")[:, 0:COLS], par("b_gate"), GATE_AT,
                                  ALU.add, ALU.is_gt).then_inc(drains(f"gate{h}"), 1)

            def a_steps(q, a):
                if q == DVE_AT["sums1"]:
                    dve.wait_ge(drains("turn"), done("turn", a))
                    sums(1, a, normA, h1)
                if q == DVE_AT["variances1"]:
                    variances(1, a, normA)
                if q == DVE_AT["high1"]:
                    high_part(1, a, normA)
                for h in (0, 1):
                    if q == DVE_AT[f"b{h}"]:
                        dve.wait_ge(fills(f"b{h}"), done(f"b{h}", a))
                        dve.wait_ge(drains(f"x{h}"), done(f"x{h}", a))
                        dve.scalar_tensor_tensor(bx[:, :], ps(f"b{h}")[:, 0:COLS], par("b_b"), xp[:, :],
                                                 ALU.add, ALU.mult).then_inc(drains(f"b{h}"), 1)
                    if q == DVE_AT[f"scan{h}"]:
                        dve.wait_ge(drains(f"b{h}"), done(f"b{h}", a))
                        dve.scalar_tensor_tensor(drive[:, :], th[:, :], 1.0, bx[:, :],
                                                 ALU.add, ALU.mult).then_inc(drive_ready, 1)
                        dve.wait_ge(drive_ready, value(a, 2, h + 1))
                        dve.wait_ge(decay_ready, value(a, 4, 2 * h + 2))
                        dve.tensor_tensor_scan(state[:, :], decay[:, :], drive[:, :], 0.0,
                                               ALU.mult, ALU.add).then_inc(scanned, 1)
                    if q == DVE_AT[f"c{h}"]:
                        dve.wait_ge(fills(f"c{h}"), done(f"c{h}", a))
                        dve.wait_ge(scanned, value(a, 2, h + 1))
                        dve.scalar_tensor_tensor(yscan[:, h, :], ps(f"c{h}")[:, 0:COLS], par("b_c"), state[:, :],
                                                 ALU.add, ALU.mult).then_inc(drains(f"c{h}"), 1)
                if q == DVE_AT["y"]:
                    dve.wait_ge(fills("y"), done("y", a))
                    dve.wait_ge(h1_by_ready, value(a, 1, 1))
                    dve.tensor_tensor(tok(h2), tok_ps("y"), tok(h1_by), ALU.add).then_inc(drains("y"), 1)
                    dve.wait_ge(drains("y"), done("y", a))
                    sums(2, a, normA, h2)
                if q == DVE_AT["variances2"]:
                    variances(2, a, normA)
                if q == DVE_AT["high2"]:
                    high_part(2, a, normA)
                if q == DVE_AT["gate0"]:
                    open_gates(0, a)

            def c_steps(q, k):
                for h in (0, 1):
                    if q != DVE_AT[f"conv{h}"]:
                        continue
                    job = f"conv{h}"
                    dve.wait_ge(odd_ready, value(k, 2, h + 1))
                    dve.tensor_tensor(conv_t[rows(h), :].rearrange("p (s t) -> p s t", s=PAIRS),
                                      conv_ps(job)[0:CH, :, 0:LEN],
                                      odd_taps[:, :].rearrange("p (s t) -> p s t", s=PAIRS), ALU.add)\
                       .then_inc(drains(job), 1)

            def b_steps(q, b):
                if q == DVE_AT["ysum"]:
                    dve.wait_ge(prod_summed, value(b, SLOTS, SLOTS))
                    dve.tensor_tensor(tok(ysum), ybank[0:LEN, :, :], over_seq("scale"), ALU.mult).then_inc(ysum_ready, 1)
                    dve.wait_ge(ysum_ready, value(b, 1, 1))
                    dve.wait_ge(h2_parked_ready, value(b, 1, 1))
                    dve.tensor_tensor(tok(h3), tok(ysum), tok(h2_parked), ALU.add).then_inc(h3_ready, 1)
                if q == DVE_AT["sums3"]:
                    dve.wait_ge(h3_ready, value(b, 1, 1))
                    sums(3, b, normB, h3)
                if q == DVE_AT["variances3"]:
                    variances(3, b, normB)
                if q == DVE_AT["high3"]:
                    high_part(3, b, normB)
                if q == DVE_AT["value"]:
                    dve.wait_ge(fills("value"), done("value", b))
                    dve.tensor_tensor(tok(val), tok_ps("value"), over_seq("b_value"), ALU.add).then_inc(drains("value"), 1)
                for h in (0, 1):
                    if q == DVE_AT[f"phase{h}"]:
                        dve.wait_ge(drains(f"phase{h}"), done(f"phase{h}", b))
                        dve.scalar_tensor_tensor(folded[:, h, :], ang[:, h, :], par("fold"), ang[:, h, :],
                                                 ALU.mult, ALU.max).then_inc(folded_ready, 1)
                if q == DVE_AT["queries"]:
                    dve.wait_ge(phase_ready, value(b, 1, 1))
                    dve.tensor_copy(qphase[:, :, :], phase[CH:P, :, :]).then_inc(qphase_ready, 1)
                for h in (0, 1):
                    if q == DVE_AT[f"score{h}"]:
                        dve.wait_ge(fills(f"score{h}"), done(f"score{h}", b))
                        dve.tensor_tensor(score[0:LEN, h, :].rearrange("t (p s) -> t p s", p=PAIRS),
                                          ps(f"score{h}")[0:LEN, 0:COLS].rearrange("t (p s) -> t p s", p=PAIRS),
                                          par("causal")[0:LEN, :].unsqueeze(1).broadcast_to([LEN, PAIRS, LEN]),
                                          ALU.mult).then_inc(drains(f"score{h}"), 1)
                if q == DVE_AT["attend"]:
                    dve.wait_ge(fills("attend"), done("attend", b))
                    dve.tensor_tensor(tok(h4), tok_ps("attend"), tok(h3), ALU.add).then_inc(drains("attend"), 1)
                    dve.wait_ge(drains("attend"), done("attend", b))
                    sums(4, b, normB, h4)
                if q == DVE_AT["variances4"]:
                    variances(4, b, normB)
                if q == DVE_AT["high4"]:
                    high_part(4, b, normB)
                for h in (0, 1):
                    if q == DVE_AT[f"up{h}"]:
                        for k in (0, 1):
                            dve.wait_ge(drains(f"up{h}{k}"), done(f"up{h}{k}", b))
                            dve.tensor_copy(hid_hi[:, h, k, :], hid[:, h, k, :]).then_inc(hid_hi_ready, 1)
                if q == DVE_AT["logits"]:
                    dve.wait_ge(fills("logits"), done("logits", b))
                    dve.tensor_tensor(tok(logit_hi), logits_ps()[:, :, 0:EXPERTS],
                                      par("b_route")[0:LEN, :].rearrange("p (s e) -> p s e", s=SEQS),
                                      ALU.add).then_inc(logit_hi_ready, 1)
                    dve.wait_ge(logit_hi_ready, value(b, 1, 1))
                    dve.tensor_tensor(tok(logit), logits_ps()[:, :, EXPERTS:], tok(logit_hi), ALU.add)\
                       .then_inc(drains("logits"), 1)
                    dve.wait_ge(drains("logits"), done("logits", b))
                    dve.tensor_reduce(tok(top), tok(logit), AX.X, ALU.max).then_inc(route_dve, 1)
                    dve.wait_ge(route_dve, value(b, 12, 1))
                    dve.tensor_tensor(tok(zed), tok(logit), over_ch(top, EXPERTS), ALU.subtract).then_inc(route_dve, 1)
                    dve.tensor_tensor(tok(equal), tok(logit), over_ch(top, EXPERTS), ALU.is_equal).then_inc(route_dve, 1)
                    dve.wait_ge(route_dve, value(b, 12, 3))
                    dve.tensor_tensor(tok(order), tok(equal), par("rank")[0:LEN, :].rearrange("p (s e) -> p s e", s=SEQS),
                                      ALU.mult).then_inc(route_dve, 1)
                    dve.wait_ge(route_dve, value(b, 12, 4))
                    dve.tensor_reduce(tok(first), tok(order), AX.X, ALU.max).then_inc(route_dve, 1)
                    dve.wait_ge(route_dve, value(b, 12, 5))
                    dve.tensor_tensor(tok(onehot), tok(order), over_ch(first, EXPERTS), ALU.is_equal).then_inc(route_dve, 1)
                if q == DVE_AT["prob"]:
                    dve.wait_ge(route_act, value(b, 1, 1))
                    dve.tensor_scalar(tok(expd), tok(zth), -1.0, 1.0, ALU.mult, ALU.add).then_inc(route_dve, 1)
                    dve.wait_ge(route_dve, value(b, 12, 7))
                    dve.reciprocal(tok(expr), tok(expd)).then_inc(route_dve, 1)
                    dve.wait_ge(route_dve, value(b, 12, 8))
                    dve.scalar_tensor_tensor(tok(expz), tok(zth), 1.0, tok(expr), ALU.add, ALU.mult).then_inc(route_dve, 1)
                    dve.wait_ge(route_dve, value(b, 12, 9))
                    dve.tensor_reduce(tok(esum), tok(expz), AX.X, ALU.add).then_inc(route_dve, 1)
                    dve.wait_ge(route_dve, value(b, 12, 10))
                    dve.reciprocal(tok(prob), tok(esum)).then_inc(route_dve, 1)
                    dve.wait_ge(route_dve, value(b, 12, 11))
                    dve.tensor_tensor(tok(gate), tok(onehot), over_ch(prob, EXPERTS), ALU.mult).then_inc(route_dve, 1)

            def d_steps(q, d):
                if q == DVE_AT["bias"]:
                    dve.wait_ge(fills("bias"), done("bias", d))
                    dve.tensor_tensor(tok(h4_bias), tok_ps("bias"), tok(h4), ALU.add).then_inc(drains("bias"), 1)
                for s in range(SEQS):
                    if q != DVE_AT[f"down{s}"]:
                        continue
                    dve.wait_ge(fills(f"down{s}"), done(f"down{s}", d))
                    if s == 0:
                        dve.wait_ge(route_dve, value(d, 12, 12))
                    dve.tensor_tensor(tok(sel[s % 2]), ps(f"down{s}")[0:LEN, :].rearrange("t (e c) -> t e c", e=EXPERTS),
                                      gate[0:LEN, s, :].unsqueeze(2).broadcast_to([LEN, EXPERTS, CH]),
                                      ALU.mult).then_inc(drains(f"down{s}"), 1)
                    dve.wait_ge(drains(f"down{s}"), done(f"down{s}", d))
                    dve.wait_ge(h5_ready, value(d, 1, 0))
                    dve.tensor_reduce(mixed[0:LEN, s, :], tok(sel[s % 2]).rearrange("t e c -> t c e"),
                                      AX.X, ALU.add).then_inc(mixed_ready, 1)

            def products(q, f):
                dve.wait_ge(wsign_ready, value(f, SLOTS, q + 1))
                dve.wait_ge(prod_summed, value(f, SLOTS, q - 1))
                if q % HALF == 0:
                    dve.wait_ge(xsign_ready, value(f, 4, 2 * (q // HALF) + 2))
                dve.tensor_tensor(prod[q % 2][:, :, 0:COLS], wsign[q % 2][:, :, :],
                                  xsign[q // HALF][:, :].unsqueeze(1).broadcast_to([P, 2, COLS]),
                                  ALU.mult).then_inc(prod_ready, 1)

            def split_weights():
                dve.wait_ge(params_landed, 16)
                dve.tensor_copy(w_hi[:, :], prm[:, SPLIT[0]:SPLIT[1]]).then_inc(setup_dve, 1)
                dve.wait_ge(setup_dve, 4)
                dve.tensor_tensor(w_lo[:, :], prm[:, SPLIT[0]:SPLIT[1]], w_hi[:, :].bitcast(F32),
                                  ALU.subtract).then_inc(setup_dve, 1)
                dve.wait_ge(setup_dve, 5)
                for part, w in enumerate((hi("w_route"), lo("w_route"))):
                    dve.tensor_copy(route_w[:, :, part * EXPERTS:(part + 1) * EXPERTS],
                                    w.rearrange("p (k e) -> p k e", k=2)).then_inc(setup_dve, 1)
                dve.tensor_copy(pair_sum[:, :], par("pair_sum")).then_inc(setup_dve, 1)

            def split_experts():
                dve.wait_ge(setup_act, 3)
                dve.wait_ge(experts_landed, 48)
                dve.tensor_tensor(ew[:, :], ew[:, :], ew_hi, ALU.subtract).then_inc(setup_dve, 1)
                dve.wait_ge(setup_dve, 9)
                dve.tensor_copy(signs_w[:, :], ew[:, :]).then_inc(setup_dve, 1)
                dve.wait_ge(setup_dve, 10)
                dve.tensor_tensor(signs_w[64:P, :], ew[64:P, :], signs_w[64:P, :], ALU.subtract).then_inc(setup_dve, 1)
                dve.tensor_copy(signs_w[0:32, :], ew_hi[0:32, :]).then_inc(setup_dve, 1)

            dve.wait_ge(conv_params_landed, 16)
            dve.tensor_tensor(taps[:, :, :], par("conv_w").rearrange("p (f k) -> p f k", f=TAPS),
                              par("filt").unsqueeze(2).broadcast_to([P, TAPS, CH]), ALU.mult).then_inc(setup_dve, 1)
            dve.wait_ge(setup_dve, 1)
            dve.tensor_copy(taps_hi[:, :, :], taps[:, :, :]).then_inc(setup_dve, 1)
            dve.wait_ge(setup_dve, 2)
            dve.tensor_tensor(taps_lo[:, :, :], taps[:, :, :], taps_hi[:, :, :].bitcast(F32),
                              ALU.subtract).then_inc(setup_dve, 1)

            def iteration(c, has_c, has_a, has_f, has_b, has_d):
                for q in range(SLOTS):
                    if has_f:
                        products(q, (c, 0))
                    for at in (q, q + 0.5):
                        if has_c and at == DVE_AT["frames"]:
                            split_frames((c, 2))
                            if isinstance(c, int) and c == -2:
                                split_weights()
                        if has_a:
                            a_steps(at, (c, 1))
                        if isinstance(c, int) and c == -1 and at == DVE_AT["high1"]:
                            split_experts()
                        if has_c:
                            c_steps(at, (c, 2))
                        if has_b:
                            b_steps(at, (c, -1))
                        if has_f and at == DVE_AT["park"]:
                            dve.wait_ge(h3_ready, value((c, 0), 1, 0))
                            dve.tensor_copy(tok(h2_parked), tok(h2)).then_inc(h2_parked_ready, 1)
                        if has_d:
                            d_steps(at, (c, -2))
                if has_a:
                    open_gates(1, (c, 1))
            schedule(dve, iteration)

        @block.gpsimd
        def _(pool):
            def centre(n, chunk, t, src):
                pool.wait_ge(norm_dve[n], value(chunk, 4, 2))
                pool.tensor_tensor(tok(t["xc"]), tok(src), over_ch(t["mean"]), ALU.subtract).then_inc(norm_pool[n], 1)

            def normalise(n, chunk, t):
                pool.wait_ge(norm_dve[n], value(chunk, 4, 4))
                pool.tensor_tensor(tok(t["rstd"]), tok(t["var"]), tok(power), ALU.pow).then_inc(norm_pool[n], 1)
                pool.wait_ge(norm_pool[n], value(chunk, 3, 2))
                pool.tensor_tensor(tok(t["xn"]), tok(t["xc"]), over_ch(t["rstd"]), ALU.mult).then_inc(norm_pool[n], 1)

            def low_part(n, chunk, t):
                pool.wait_ge(parts_hi_ready[n], value(chunk, 1, 1))
                pool.wait_ge(norm_pool[n], value(chunk, 3, 3))
                pool.tensor_tensor(t["parts"][0:LEN, :, 1, :], tok(t["xn"]), t["parts"][0:LEN, :, 0, :],
                                   ALU.subtract).then_inc(parts_lo_ready[n], 1)

            def split_frames(a):
                pool.wait_ge(frames_hi_ready, value(a, 1, 1))
                pool.tensor_tensor(frames_lo[:, :, :], frames[:, :, :], frames_hi[:, :, :].bitcast(F32),
                                   ALU.subtract).then_inc(frames_lo_ready, 1)

            def a_steps(q, a):
                if q == POOL_AT["centre1"]:
                    centre(1, a, normA, h1)
                    pool.tensor_tensor(tok(h1_by), tok(h1), over_seq("b_y"), ALU.add).then_inc(h1_by_ready, 1)
                if q == POOL_AT["normalise1"]:
                    normalise(1, a, normA)
                if q == POOL_AT["low1"]:
                    low_part(1, a, normA)
                for h in (0, 1):
                    if q == POOL_AT[f"delta{h}"]:
                        pool.wait_ge(drains(f"delta{h}"), done(f"delta{h}", a))
                        stand_alone(pool)
                        pool.tensor_scalar(decay[:, :], th[:, :], -0.5, 0.5, ALU.mult, ALU.add).then_inc(decay_ready, 1)
                        pool.wait_ge(decay_ready, value(a, 4, 2 * h + 1))
                        stand_alone(pool)
                        pool.memset(decay[:, :].rearrange("p (s t) -> p s t", t=LEN)[:, :, 0:1], 0.0)\
                            .then_inc(decay_ready, 1)
                if q == POOL_AT["centre2"]:
                    centre(2, a, normA, h2)
                if q == POOL_AT["normalise2"]:
                    normalise(2, a, normA)
                if q == POOL_AT["low2"]:
                    low_part(2, a, normA)

            def b_steps(q, b):
                if q == POOL_AT["centre3"]:
                    centre(3, b, normB, h3)
                if q == POOL_AT["normalise3"]:
                    normalise(3, b, normB)
                if q == POOL_AT["low3"]:
                    low_part(3, b, normB)
                if q == POOL_AT["centre4"]:
                    centre(4, b, normB, h4)
                if q == POOL_AT["normalise4"]:
                    normalise(4, b, normB)
                if q == POOL_AT["low4"]:
                    low_part(4, b, normB)
                for h in (0, 1):
                    if q == POOL_AT[f"up{h}"]:
                        for k in (0, 1):
                            pool.wait_ge(hid_hi_ready, value(b, 4, 2 * h + k + 1))
                            pool.tensor_tensor(hid_lo[:, h, k, :], hid[:, h, k, :], hid_hi[:, h, k, :].bitcast(F32),
                                               ALU.subtract).then_inc(hid_lo_ready, 1)

            def d_steps(q, d):
                if q == POOL_AT["h5"]:
                    pool.wait_ge(drains("bias"), done("bias", d))
                    pool.wait_ge(mixed_ready, value(d, SEQS, SEQS))
                    pool.wait_ge(stored, value(d, 16, 0))
                    pool.tensor_tensor(tok(h5), tok(h4_bias), tok(mixed), ALU.add).then_inc(h5_ready, 1)

            pool.memset(ew[:, :], 0.0).then_inc(ew_zeroed, 1)
            pool.memset(power[:, :], -0.5).then_inc(setup_pool, 1)
            for i in (0, 1):
                pool.memset(prod[i][:, :, COLS:ZCOLS], 0.0).then_inc(setup_pool, 1)
            pool.wait_ge(setup_pool, SETUP_POOL)

            def iteration(c, has_c, has_a, has_f, has_b, has_d):
                if isinstance(c, int) and c == -1:
                    pool.wait_ge(params_landed, 16)
                for q in range(SLOTS):
                    for at in (q, q + 0.5):
                        if has_c and at == POOL_AT["frames"]:
                            split_frames((c, 2))
                        if has_a:
                            a_steps(at, (c, 1))
                        if has_d:
                            d_steps(at, (c, -2))
                        if has_b:
                            b_steps(at, (c, -1))

            schedule(pool, iteration)


def packed_parameters(w):
    f = {k: np.asarray(v, np.float32) for k, v in w.items()}
    pk = np.zeros((P, PACKED), np.float32)

    def put(name, a, r0=0, c0=0):
        a = np.asarray(a, np.float32)
        pk[r0:r0 + a.shape[0], AT[name][0] + c0:AT[name][0] + c0 + a.shape[1]] = a

    def row(name, v, n=1):
        put(name, np.tile(v.reshape(1, -1), (P, n)))

    def both(name, a):
        put(name, np.tile(a, (2, 1)))

    put("conv_w", f["L0_tok_W_k"].reshape(TAPS, DIM, CH).transpose(1, 0, 2).reshape(DIM, -1))
    put("filt", f["L0_tok_filt"].T)
    both("conv_b", f["L0_tok_b_k"].reshape(-1, 1))
    both("w_x", f["L0_attn_Wx"])
    both("w_b", f["L0_attn_Wbc"][:, :STATE])
    both("w_c", f["L0_attn_Wbc"][:, STATE:])
    both("w_delta", f["L0_attn_Wd"])
    put("b_x", f["L0_attn_bx"].reshape(-1, 1))
    put("b_b", f["L0_attn_bbc"][:STATE].reshape(-1, 1))
    put("b_c", f["L0_attn_bbc"][STATE:].reshape(-1, 1))
    put("b_delta", f["L0_attn_bd"].reshape(-1, 1))
    put("w_y", f["L0_attn_Wy"])
    row("b_y", f["L0_attn_by"])
    for part in range(3):
        for h in (0, 1):
            put("w_gate", f["L0_ffn_proj_w"].T, CH * h, 32 * part)
        put("b_gate", f["L0_ffn_proj_b"].reshape(-1, 1), 32 * part)
    row("scale", f["L0_ffn_scale"])
    both("w_enc", np.concatenate([f["L1_attn_kw1"].T, f["L1_attn_qw1"].T], 1))
    put("b_enc", np.concatenate([f["L1_attn_kb1"], f["L1_attn_qb1"]]).reshape(-1, 1))
    for i, n in enumerate("kq"):
        for twice in (0, 1):
            put("w_phase", f[f"L1_attn_{n}w2"].T, CH * i, CH * i + PHASES * twice)
            put("b_phase", f[f"L1_attn_{n}b2"].reshape(-1, 1), CH * i + PHASES * twice)
    both("w_value", f["L1_attn_vw"].T)
    row("b_value", f["L1_attn_vb"])
    both("w_up", f["L1_ffn_W1"])
    put("b_up", f["L1_ffn_b1"].reshape(2, P).T)
    put("w_route", f["L1_ffn_Wg"].reshape(2, P, EXPERTS).transpose(1, 0, 2).reshape(P, -1))
    row("b_route", f["L1_ffn_bg"], SEQS)
    put("w_down", f["L1_ffn_Wd"].reshape(EXPERTS, 2, P, CH).transpose(2, 1, 0, 3).reshape(P, -1))
    for s in range(SEQS):
        put("b_down", f["L1_ffn_bd"], EXPERTS * s, CH * s)
    put("ident", np.eye(P))
    t = np.arange(1, LEN + 1)
    put("causal", np.triu(np.ones((LEN, LEN))) / np.sqrt(t * PHASES)[None, :])
    put("pair_sum", np.repeat(np.eye(2), CH, axis=0))
    cosine = np.arange(P) % CH < PHASES
    put("fold", np.where(cosine, -1.0, 1.0).reshape(-1, 1))
    put("sin_scale", np.where(cosine, -math.pi, math.pi).reshape(-1, 1))
    put("sin_bias", np.where(cosine, math.pi / 2, 0.0).reshape(-1, 1))
    row("rank", np.arange(EXPERTS, 0, -1, dtype=np.float32), SEQS)
    return pk


def kernel(**inputs):
    import concourse.bacc as bacc
    from concourse.bass_utils import run_bass_kernel_spmd

    a = {k: np.asarray(v) for k, v in inputs.items()}
    weight = a["L0_ffn_weight"]
    arrays = {
        "x_dram": np.ascontiguousarray(a["x"].transpose(2, 0, 1)),
        "params_dram": packed_parameters({k: v for k, v in a.items() if k != "x"}),
        "experts_dram": np.ascontiguousarray(weight[0].transpose(0, 2, 1).reshape(EXPERTS, CH * CH)),
    }
    nc = bacc.Bacc("TRN2", target_bir_lowering=False, num_devices=1)
    args = [nc.dram_tensor(n, v.shape, mybir.dt.from_np(v.dtype), kind="ExternalInput").ap() for n, v in arrays.items()]
    out = nc.dram_tensor("out_dram", (LEN, BATCH, CH), F32, kind="ExternalOutput").ap()
    tower(nc, *args, out)
    r = run_bass_kernel_spmd(nc, [arrays], core_ids=[0])
    return np.ascontiguousarray(r.results[0]["out_dram"].transpose(1, 0, 2))
```
